# Optimizing a Trainium2 kernel written in Bass

```python
import numpy as np
import jax
import jax.numpy as jnp

def _softmax(x, axis=-1):
    return jax.nn.softmax(x, axis=axis)

def _gelu(x):
    return jax.nn.gelu(x, approximate=True)

def _silu(x):
    return jax.nn.silu(x)

def _sigmoid(x):
    return jax.nn.sigmoid(x)

def _layernorm(x, axis=-1, eps=1e-05):
    m = jnp.mean(x, axis=axis, keepdims=True)
    v = jnp.var(x, axis=axis, keepdims=True)
    return (x - m) / jnp.sqrt(v + eps)

def _scatter_add(tgt, idx, src, axis=0):
    return tgt.at[idx].add(src)

def _segment_sum(src, seg, n):
    return jax.ops.segment_sum(src, seg, n)
kernel_name = 'mk_early_fusion_d1_tok_img512_r4_26c928'

def setup_inputs(seed: int=0):
    np.random.seed(seed)
    _w = jnp.asarray

    def _rec_inputs():
        import jax
        import jax.numpy as jnp
        _rk = jax.random.key(seed)
        x = -0.000477451 + 1.00034 * jax.random.normal(jax.random.fold_in(_rk, 1), (8, 32, 32, 29), jnp.float32)
        txt = 0.228173 + 0.721734 * jax.random.normal(jax.random.fold_in(_rk, 2), (8, 128, 128), jnp.float32)
        return (x, txt)
    x, txt = _rec_inputs()

    def _L0_tok_setup():
        import jax, jax.numpy as jnp
        import numpy as np
        import math
        H, W_DIM, D_MODEL, B = (32, 32, 128, 128)
        F_TOTAL = 29
        SEQ_LEN = H * W_DIM

        def make_pe(seq_len: int, d_model: int) -> jnp.ndarray:
            position = np.arange(seq_len, dtype=np.float32)[:, None]
            div_term = np.exp(np.arange(0, d_model, 2, dtype=np.float32) * (-math.log(10000.0) / d_model))
            pe = np.zeros((seq_len, d_model), dtype=np.float32)
            pe[:, 0::2] = np.sin(position * div_term)
            pe[:, 1::2] = np.cos(position * div_term)
            return jnp.asarray(pe)
        key = jax.random.key(seed)
        k1, k2 = jax.random.split(key)
        state_tensor = jax.random.normal(k1, (B, H, W_DIM, F_TOTAL), dtype=jnp.float32)
        W = jax.random.normal(k2, (F_TOTAL, D_MODEL), dtype=jnp.float32) * 0.05
        return {'state_tensor': state_tensor, 'W': W}
    _L0_tok_all = _L0_tok_setup()
    _L0_tok_in = {k: v for k, v in _L0_tok_all.items() if k in ('W',)}
    del _L0_tok_all

    def _L0_attn_setup():
        import jax, jax.numpy as jnp
        import numpy as np
        NUM_HEADS = 8
        EPS = 1e-06

        def _fourier_attention(x, w_qkv, w_proj, b_proj, paramR):
            B, N, C = x.shape
            H = NUM_HEADS
            Dh = C // H
            qkv = jnp.einsum('bnc,kc->bnk', x, w_qkv).reshape(B, N, 3, H, Dh)
            q = qkv[:, :, 0].transpose(0, 2, 1, 3)
            k = qkv[:, :, 1].transpose(0, 2, 1, 3)
            v = qkv[:, :, 2].transpose(0, 2, 1, 3)
            R = paramR[0]
            diff = q[:, :, :, None, :] - k[:, :, None, :, :]
            near0 = jnp.abs(diff) < 1e-08
            safe = jnp.where(near0, jnp.float32(1.0), diff)
            s = jnp.where(near0, R, jnp.sin(R * safe) / safe)
            score = jnp.prod(s, axis=-1)
            a4 = score ** 4
            attn = a4 / (jnp.sum(a4, axis=-1, keepdims=True) + EPS)
            out = jnp.einsum('bhqk,bhkd->bhqd', attn, v)
            out = out.transpose(0, 2, 1, 3).reshape(B, N, C)
            return jnp.einsum('bnc,oc->bno', out, w_proj) + b_proj
        key = jax.random.key(seed)
        k1, k2, k3 = jax.random.split(key, 3)
        B, N, C = (4, 64, 128)
        x = jax.random.normal(k1, (B, N, C), dtype=jnp.float32)
        w_qkv = jax.random.normal(k2, (3 * C, C), dtype=jnp.float32) * C ** (-0.5)
        w_proj = jax.random.normal(k3, (C, C), dtype=jnp.float32) * C ** (-0.5)
        b_proj = jnp.zeros((C,), dtype=jnp.float32)
        paramR = jnp.ones((1,), dtype=jnp.float32)
        return {'x': x, 'w_qkv': w_qkv, 'w_proj': w_proj, 'b_proj': b_proj, 'paramR': paramR}
    _L0_attn_all = _L0_attn_setup()
    _L0_attn_in = {k: v for k, v in _L0_attn_all.items() if k in ('w_qkv', 'w_proj', 'b_proj', 'paramR')}
    del _L0_attn_all

    def _L0_ffn_setup():
        import jax, jax.numpy as jnp
        import numpy as np
        MICRO_BATCHES = 2
        TOP_K = 2
        D = 128
        E = 8
        B, S = (8, 2048)
        key = jax.random.key(seed)
        ks = jax.random.split(key, 12)
        s = 0.02
        return {'x': jax.random.normal(ks[0], (B, S, D), dtype=jnp.float32), 'ln_g': jnp.ones((D,), jnp.float32), 'ln_b': jnp.zeros((D,), jnp.float32), 'attn_w': jax.random.normal(ks[1], (D, D), jnp.float32) * s, 'attn_b': jnp.zeros((D,), jnp.float32), 'gate_w': jax.random.normal(ks[2], (E, D), jnp.float32) * s, 'fc1_w': jax.random.normal(ks[3], (E, 4 * D, D), jnp.float32) * s, 'fc1_b': jnp.zeros((E, 4 * D), jnp.float32), 'fc2_w': jax.random.normal(ks[4], (E, D, 4 * D), jnp.float32) * s, 'fc2_b': jnp.zeros((E, D), jnp.float32), 'next_w': jax.random.normal(ks[5], (D, D), jnp.float32) * s, 'next_b': jnp.zeros((D,), jnp.float32)}
    _L0_ffn_all = _L0_ffn_setup()
    _L0_ffn_in = {k: v for k, v in _L0_ffn_all.items() if k in ('ln_g', 'ln_b', 'attn_w', 'attn_b', 'gate_w', 'fc1_w', 'fc1_b', 'fc2_w', 'fc2_b', 'next_w', 'next_b')}
    del _L0_ffn_all
    return {'x': x, 'txt': txt, 'L0_tok_W': _L0_tok_in['W'], 'L0_attn_w_qkv': _L0_attn_in['w_qkv'], 'L0_attn_w_proj': _L0_attn_in['w_proj'], 'L0_attn_b_proj': _L0_attn_in['b_proj'], 'L0_attn_paramR': _L0_attn_in['paramR'], 'L0_ffn_ln_g': _L0_ffn_in['ln_g'], 'L0_ffn_ln_b': _L0_ffn_in['ln_b'], 'L0_ffn_attn_w': _L0_ffn_in['attn_w'], 'L0_ffn_attn_b': _L0_ffn_in['attn_b'], 'L0_ffn_gate_w': _L0_ffn_in['gate_w'], 'L0_ffn_fc1_w': _L0_ffn_in['fc1_w'], 'L0_ffn_fc1_b': _L0_ffn_in['fc1_b'], 'L0_ffn_fc2_w': _L0_ffn_in['fc2_w'], 'L0_ffn_fc2_b': _L0_ffn_in['fc2_b'], 'L0_ffn_next_w': _L0_ffn_in['next_w'], 'L0_ffn_next_b': _L0_ffn_in['next_b']}

def reference(x, txt, L0_tok_W, L0_attn_w_qkv, L0_attn_w_proj, L0_attn_b_proj, L0_attn_paramR, L0_ffn_ln_g, L0_ffn_ln_b, L0_ffn_attn_w, L0_ffn_attn_b, L0_ffn_gate_w, L0_ffn_fc1_w, L0_ffn_fc1_b, L0_ffn_fc2_w, L0_ffn_fc2_b, L0_ffn_next_w, L0_ffn_next_b):
    import jax
    import jax.numpy as jnp

    def _L0_tok_ref(state_tensor, W):
        import jax, jax.numpy as jnp
        import numpy as np
        import math
        H, W_DIM, D_MODEL, B = (32, 32, 128, 128)
        F_TOTAL = 29
        SEQ_LEN = H * W_DIM

        def make_pe(seq_len: int, d_model: int) -> jnp.ndarray:
            position = np.arange(seq_len, dtype=np.float32)[:, None]
            div_term = np.exp(np.arange(0, d_model, 2, dtype=np.float32) * (-math.log(10000.0) / d_model))
            pe = np.zeros((seq_len, d_model), dtype=np.float32)
            pe[:, 0::2] = np.sin(position * div_term)
            pe[:, 1::2] = np.cos(position * div_term)
            return jnp.asarray(pe)
        b, h, w, f = state_tensor.shape
        s = h * w
        x = state_tensor.reshape(b, s, f)
        emb = jnp.einsum('bsf,fd->bsd', x, W)
        pe = make_pe(s * 2, W.shape[1])[:s]
        return emb + pe[None, :, :]

    def _L0_attn_ref(x, w_qkv, w_proj, b_proj, paramR):
        import jax, jax.numpy as jnp
        import numpy as np
        NUM_HEADS = 8
        EPS = 1e-06

        def _fourier_attention(x, w_qkv, w_proj, b_proj, paramR):
            B, N, C = x.shape
            H = NUM_HEADS
            Dh = C // H
            qkv = jnp.einsum('bnc,kc->bnk', x, w_qkv).reshape(B, N, 3, H, Dh)
            q = qkv[:, :, 0].transpose(0, 2, 1, 3)
            k = qkv[:, :, 1].transpose(0, 2, 1, 3)
            v = qkv[:, :, 2].transpose(0, 2, 1, 3)
            R = paramR[0]
            diff = q[:, :, :, None, :] - k[:, :, None, :, :]
            near0 = jnp.abs(diff) < 1e-08
            safe = jnp.where(near0, jnp.float32(1.0), diff)
            s = jnp.where(near0, R, jnp.sin(R * safe) / safe)
            score = jnp.prod(s, axis=-1)
            a4 = score ** 4
            attn = a4 / (jnp.sum(a4, axis=-1, keepdims=True) + EPS)
            out = jnp.einsum('bhqk,bhkd->bhqd', attn, v)
            out = out.transpose(0, 2, 1, 3).reshape(B, N, C)
            return jnp.einsum('bnc,oc->bno', out, w_proj) + b_proj
        return _fourier_attention(x, w_qkv, w_proj, b_proj, paramR)

    def _L0_ffn_ref(x, ln_g, ln_b, attn_w, attn_b, gate_w, fc1_w, fc1_b, fc2_w, fc2_b, next_w, next_b):
        import jax, jax.numpy as jnp
        import numpy as np
        MICRO_BATCHES = 2
        TOP_K = 2
        D = 128
        E = 8
        B, S = (8, 2048)
        b, s, d = x.shape
        xf = x.reshape(b * s, d)
        mu = jnp.mean(xf, axis=-1, keepdims=True)
        var = jnp.var(xf, axis=-1, keepdims=True)
        normed = (xf - mu) / jnp.sqrt(var + 1e-05) * ln_g + ln_b
        x_attn = normed @ attn_w.T + attn_b + xf
        logits = x_attn @ gate_w.T
        _scores, _indices = jax.lax.top_k(logits, TOP_K)
        e = fc1_w.shape[0]
        t = b * s // (MICRO_BATCHES * e)
        tok = x_attn.reshape(MICRO_BATCHES, e, t, d)
        h = jnp.einsum('meti,ehi->meth', tok, fc1_w) + fc1_b[None, :, None, :]
        h = jax.nn.gelu(h, approximate=False)
        y = jnp.einsum('meth,edh->metd', h, fc2_w) + fc2_b[None, :, None, :]
        yf = y.reshape(b * s, d)
        out = jax.nn.gelu(yf @ next_w.T + next_b, approximate=False)
        return out.reshape(b, s, d)
    h = _L0_tok_ref(x, L0_tok_W)
    h = jnp.concatenate([h, txt], axis=1)
    h = h + _L0_attn_ref(_layernorm(h, axis=-1), L0_attn_w_qkv, L0_attn_w_proj, L0_attn_b_proj, L0_attn_paramR)
    h = h + _L0_ffn_ref(_layernorm(h, axis=-1), L0_ffn_ln_g, L0_ffn_ln_b, L0_ffn_attn_w, L0_ffn_attn_b, L0_ffn_gate_w, L0_ffn_fc1_w, L0_ffn_fc1_b, L0_ffn_fc2_w, L0_ffn_fc2_b, L0_ffn_next_w, L0_ffn_next_b)
    return h

_drawn_inputs = setup_inputs


def setup_inputs(seed=0):
    import zlib

    import numpy as np

    out = dict(_drawn_inputs(seed))
    spreads = {'L0_attn_b_proj': (0.0, 0.1),
     'L0_ffn_ln_g': (1.0, 0.6),
     'L0_ffn_ln_b': (0.0, 0.8),
     'L0_ffn_attn_b': (0.0, 0.8),
     'L0_ffn_fc1_b': (0.0, 0.8),
     'L0_ffn_fc2_b': (0.0, 0.731),
     'L0_ffn_next_b': (0.0, 0.8)}
    factors = {'L0_ffn_attn_w': 8.0, 'L0_ffn_fc1_w': 8.0, 'L0_ffn_fc2_w': 7.988, 'L0_ffn_next_w': 4.201}
    for name, (base, spread) in spreads.items():
        noise = np.random.default_rng([zlib.crc32(name.encode()), seed]).standard_normal(out[name].shape)
        drawn = base * np.exp(spread * noise) if base else spread * noise
        out[name] = jnp.asarray(drawn.astype(out[name].dtype))
    for name, factor in factors.items():
        out[name] = (out[name] * factor).astype(out[name].dtype)
    return out
```

```python
from contextlib import ExitStack
from math import comb, log, pi

import concourse.bass as bass
import numpy as np
from concourse import mybir

ALU = mybir.AluOpType
ACT = mybir.ActivationFunctionType
AX = mybir.AxisListType
F32 = mybir.dt.float32
F16 = mybir.dt.float16
I32 = mybir.dt.int32

BATCH, IMG, FEAT, TXT, C = 8, 1024, 29, 128, 128
N = IMG + TXT
P = 128
KT = N // P
HEADS, DH = 8, 16
VW = DH + 1
QC = 384
NQ = N // QC
KG = 3
UNITS = NQ * KT // KG
BH = BATCH * HEADS
EXPERTS, HID, MICRO = 8, 512, 2
SEG = BATCH * N // (MICRO * EXPERTS)
EPS_LN = 1e-5
EPS_ATT = 1e-6
NEAR = 1e-8

DIRICHLET = 6
REACH = 6.25
RMAX = 8.0
DEGREE = 9
RANK = 7
POWERS = 2 * DEGREE
PB = 6
PROWS = PB * DH
LROWS = RANK * DH + 2
PAIRS = DH // 2
WAVES = 2 * 3 * 3
PF = 2 * WAVES
TP = 3
NT = -(-PAIRS // TP)
AROWS = TP * PF
GSCALE = 2.0 ** 14
LSCALE = 2.0 ** 11
MAGIC = 1.5 * 2.0 ** 23
KBASE = 32
SLOTS = 9
LPOS = 4
LN = 12
GPOS = [p for p in range(SLOTS) if p != LPOS]


def exponent_tables():
    span = 2 * REACH
    t = np.cos(np.pi * (np.arange(4000) + 0.5) / 4000)
    u = (t + 1) / 2 * span * span
    f = 4 * np.log(np.sinc(np.sqrt(u) / DIRICHLET / np.pi))
    cheb = np.polynomial.chebyshev.chebfit(t, f / u, DEGREE - 1)
    poly = np.polynomial.Polynomial(np.polynomial.chebyshev.cheb2poly(cheb))
    coef = poly(np.polynomial.Polynomial([-1, 2])).coef
    both = np.zeros((POWERS + 1, POWERS + 1))
    for m in range(1, DEGREE + 1):
        for i in range(2 * m + 1):
            both[i, 2 * m - i] += span ** 2 * coef[m - 1] / 4 ** m * comb(2 * m, i) * (-1) ** i
    x = np.cos(np.pi * (np.arange(60) + 0.5) / 60)
    grid = x[:, None] ** np.arange(1, POWERS + 1)
    u_, s, v = np.linalg.svd(grid @ both[1:, 1:] @ grid.T)
    left = np.linalg.lstsq(grid, u_[:, :RANK] * np.sqrt(s[:RANK]), rcond=None)[0]
    right = np.linalg.lstsq(grid, v[:RANK].T * np.sqrt(s[:RANK]), rcond=None)[0]
    return left, right, both[1:, 0], both[0, 1:]


def shape_constants():
    position = np.arange(IMG, dtype=np.float32)[:, None]
    div = np.exp(np.arange(0, C, 2, dtype=np.float32) * np.float32(-log(10000.0) / C))
    pe = np.zeros((IMG, C), np.float32)
    pe[:, 0::2] = np.sin(position * div)
    pe[:, 1::2] = np.cos(position * div)
    angles = np.zeros((KBASE + VW, NT, AROWS), np.float32)
    for pair in range(PAIRS):
        for w in range(WAVES):
            a, b = (1, 3, 5)[w % 3], (1, 3, 5)[w // 3 % 3] * (1 if w < 9 else -1)
            for phase in range(2):
                col = pair % TP * PF + 2 * w + phase
                for base in (0, KBASE):
                    angles[base + 2 * pair, pair // TP, col] = a / DIRICHLET / (2 * pi)
                    angles[base + 2 * pair + 1, pair // TP, col] = b / DIRICHLET / (2 * pi)
                    angles[base + DH, pair // TP, col] = 0.25 * phase
    left, right, own_q, own_k = exponent_tables()
    project = np.zeros((PROWS, 2, POWERS // PB, LROWS))
    for power in range(POWERS):
        for d in range(DH):
            row = power % PB * DH + d
            for side, (table, own) in enumerate(((left, own_q), (right, own_k))):
                for r in range(RANK):
                    project[row, side, power // PB, r * DH + d] = table[power, r] * LSCALE
                project[row, side, power // PB, RANK * DH + side] = own[power] * LSCALE
    lift = np.zeros((LROWS, 2), np.float32)
    lift[RANK * DH + 1, 0] = lift[RANK * DH, 1] = LSCALE
    bits = np.zeros((PROWS, 6), np.float32)
    for row in range(PROWS):
        for b in range(3):
            bits[row, b] = (row // DH + 1) >> b & 1
            bits[row, 3 + b] = 1 - bits[row, b]
    heads = np.kron(np.eye(HEADS), np.ones((1, DH)))
    return {
        "pe": np.ascontiguousarray(pe.reshape(KT - 1, P, C).transpose(1, 0, 2)),
        "angles": angles, "project": project.astype(np.float32), "lift": lift, "bits": bits,
        "ident": np.eye(P, dtype=np.float32), "heads": heads.astype(np.float32),
    }


def tokens_and_qkv(nc, A, S):
    with ExitStack() as ctx:
        sb = lambda name, shape, dt=F32: ctx.enter_context(nc.sbuf_tensor(name, shape, dt))
        sem = lambda name: ctx.enter_context(nc.semaphore(name))
        xT = sb("a_xT", [FEAT, IMG])
        w_tok = sb("a_wtok", [FEAT, C])
        wqkv = sb("a_wqkv", [P, 3 * C])
        pe_sb = sb("a_pe", [P, KT - 1, C])
        ident = sb("a_ident", [P, P])
        h = sb("a_h", [P, KT, C])
        xc = sb("a_xc", [P, KT, C])
        sq = sb("a_sq", [P, KT, C])
        st = sb("a_stat", [P, 6, KT])
        xnT = sb("a_xnT", [P, N])
        qk = sb("a_qk", [P, 2, N])
        va = sb("a_va", [P, HEADS, KT, VW])
        ext = sb("a_ext", [P, 4])
        row = sb("a_row", [1, 8])
        tok_ps = ctx.enter_context(nc.psum_tensor("a_tok_ps", [P, 2, 512], F32))
        x_ps = ctx.enter_context(nc.psum_tensor("a_x_ps", [P, NQ, 512], F32))
        q_ps = ctx.enter_context(nc.psum_tensor("a_q_ps", [P, NQ, 512], F32))
        consts_in, x_in, txt_in = sem("a_consts_in"), sem("a_x_in"), sem("a_txt_in")
        tok_made, h_made, ln, xn_turned, xnT_made = sem("a_tok_made"), sem("a_h_made"), sem("a_ln"), sem("a_xn_turned"), sem("a_xnT_made")
        qkv_made, q_out, k_out, v_out, ones_set = sem("a_qkv_made"), sem("a_q_out"), sem("a_k_out"), sem("a_v_out"), sem("a_ones_set")
        rooted = sem("a_rooted")
        stored, ranged, turned, flagged = sem("a_stored"), sem("a_ranged"), sem("a_turned"), sem("a_flagged")
        STORES = 4

        tok_flat = tok_ps[:].rearrange("p a (t c) -> p (a t) c", c=C)
        xT_ps = x_ps[:].rearrange("p a (t c) -> p (a t) c", c=C)

        with nc.Block() as block:
            @block.sync
            def _(sp):
                sp.dma_start(w_tok[:], A["tok_w"]).then_inc(consts_in, 16)
                sp.dma_start(wqkv[:], A["wqkvT"]).then_inc(consts_in, 16)
                sp.dma_start(pe_sb[:], A["pe"]).then_inc(consts_in, 16)
                sp.dma_start(ident[:], A["ident"]).then_inc(consts_in, 16)
                sp.dma_start(row[0:1, 0:1], A["R"]).then_inc(consts_in, 16)

                def loads(b):
                    sp.dma_start(xT[:], A["xT"][bass.ds(b, 1)].rearrange("o f s -> (o f) s")).then_inc(x_in, 16)
                    sp.dma_start(h[:, KT - 1, :], A["txt"][bass.ds(b, 1)].rearrange("o s c -> (o s) c")).then_inc(txt_in, 16)

                def stores(b):
                    one = lambda ap: ap[bass.ds(b, 1)]
                    sp.wait_ge(q_out, b + 1)
                    sp.dma_start(one(S["q"]).rearrange("o r n -> (o r) n"), qk[:, 0, :]).then_inc(stored, 16)
                    sp.wait_ge(k_out, b + 1)
                    sp.dma_start(one(S["k"]).rearrange("o r n -> (o r) n"), qk[:, 1, :]).then_inc(stored, 16)
                    sp.dma_start(one(S["h"]).rearrange("o p t c -> (o p) t c"), h[:]).then_inc(stored, 16)
                    sp.wait_ge(v_out, b + 1)
                    sp.dma_start(one(S["v"]).rearrange("o h p t v -> p (o h) (t v)"),
                                 va[:].rearrange("p h t v -> p h (t v)")).then_inc(stored, 16)

                loads(0)
                stores(0)
                with sp.Fori(1, BATCH) as b:
                    sp.wait_ge(tok_made, b)
                    sp.wait_ge(stored, b * 16 * STORES)
                    loads(b)
                    stores(b)
                sp.wait_ge(stored, BATCH * 16 * STORES)
                for what in ("q", "k"):
                    sp.dma_start(S[what][BATCH:BATCH + 1, 0:DH, :], S[what][0:1, 0:DH, :]).then_inc(stored, 16)
                sp.dma_start(S["v"][BATCH:BATCH + 1, 0:1], S["v"][0:1, 0:1]).then_inc(stored, 16)
                sp.wait_ge(stored, (BATCH * STORES + 3) * 16)

            @block.tensor
            def _(pe):
                pe.wait_ge(consts_in, 5 * 16)

                def batch(b, first):
                    pe.wait_ge(x_in, (b + 1) * 16)
                    if not first:
                        pe.wait_ge(h_made, b)
                    for t in range(KT - 1):
                        last = nc.tensor.matmul(tok_flat[:, t, :], xT[:, t * P:(t + 1) * P], w_tok[:], start=True, stop=True)
                    last.then_inc(tok_made, 1)
                    pe.wait_ge(ln, (b + 1) * LN)
                    if not first:
                        pe.wait_ge(k_out, b)
                    for t in range(KT):
                        last = nc.tensor.transpose(xT_ps[:, t, :], xc[:, t, :], ident[:])
                    last.then_inc(xn_turned, 1)
                    pe.wait_ge(xnT_made, b + 1)
                    if not first:
                        pe.wait_ge(v_out, b)
                    for i in range(NQ):
                        last = nc.tensor.matmul(q_ps[:, i, 0:QC], wqkv[:, 0:C], xnT[:, i * QC:(i + 1) * QC], start=True, stop=True)
                    last.then_inc(qkv_made, 1)
                    for i in range(NQ):
                        last = nc.tensor.matmul(x_ps[:, i, 0:QC], wqkv[:, C:2 * C], xnT[:, i * QC:(i + 1) * QC], start=True, stop=True)
                    last.then_inc(qkv_made, 1)
                    pe.wait_ge(q_out, b + 1)
                    for t in range(KT):
                        last = nc.tensor.matmul(q_ps[:, t // 3, t % 3 * P:(t % 3 + 1) * P], xnT[:, t * P:(t + 1) * P],
                                                wqkv[:, 2 * C:3 * C], start=True, stop=True)
                    last.then_inc(qkv_made, 1)

                batch(0, True)
                with pe.Fori(1, BATCH) as b:
                    batch(b, False)
                pe.wait_ge(ranged, 2 * BATCH + 2)
                pe.wait_ge(h_made, BATCH)
                nc.tensor.transpose(tok_flat[0:1, 0, :], ext[:, 0:1], ident[:]).then_inc(turned, 1)

            @block.vector
            def _(dve):
                dve.memset(ext[:], 0.0).then_inc(ranged, 1)
                dve.memset(va[:], 1.0).then_inc(ones_set, 1)
                dve.wait_ge(consts_in, 5 * 16)

                def batch(b, first):
                    dve.wait_ge(tok_made, b + 1)
                    if not first:
                        dve.wait_ge(stored, b * 16 * STORES)
                    nc.vector.tensor_tensor(h[:, 0:KT - 1, :], tok_flat[:], pe_sb[:], ALU.add).then_inc(h_made, 1)
                    dve.wait_ge(h_made, b + 1)
                    dve.wait_ge(txt_in, (b + 1) * 16)
                    if not first:
                        dve.wait_ge(xn_turned, b)
                    layernorm(dve, nc, h, xc, sq, st, ln, rooted, b * LN, b)
                    dve.wait_ge(qkv_made, 3 * b + 2)
                    nc.vector.tensor_copy(qk[:, 1, :].rearrange("p (i n) -> p i n", i=NQ), x_ps[:, :, 0:QC]).then_inc(k_out, 1)
                    dve.wait_ge(k_out, b + 1)
                    dve.wait_ge(q_out, b + 1)
                    flat = qk[:].rearrange("p s n -> p (s n)")
                    nc.vector.tensor_reduce(ext[:, 1:2], flat, AX.X, ALU.max).then_inc(ranged, 1)
                    nc.vector.tensor_reduce(ext[:, 2:3], flat, AX.X, ALU.min).then_inc(ranged, 1)
                    dve.wait_ge(ranged, 2 * b + 3)
                    nc.vector.scalar_tensor_tensor(ext[:, 3:4], ext[:, 2:3], -1.0, ext[:, 1:2], ALU.mult, ALU.max).then_inc(ones_set, 1)
                    dve.wait_ge(ones_set, 2 * b + 2)
                    nc.vector.tensor_tensor(ext[:, 0:1], ext[:, 0:1], ext[:, 3:4], ALU.max).then_inc(ones_set, 1)

                batch(0, True)
                with dve.Fori(1, BATCH) as b:
                    batch(b, False)
                dve.wait_ge(ones_set, 2 * BATCH + 1)
                dve.drain().then_inc(ranged, 1)
                dve.wait_ge(turned, 1)
                nc.vector.tensor_reduce(row[:, 1:2], tok_flat[0:1, 0, :], AX.X, ALU.max).then_inc(flagged, 1)
                nc.vector.scalar_tensor_tensor(row[:, 2:3], row[:, 0:1], -1.0, row[:, 0:1], ALU.mult, ALU.max).then_inc(flagged, 1)
                dve.wait_ge(flagged, 2)
                nc.vector.tensor_scalar(row[:, 3:4], row[:, 1:2], row[:, 2:3], REACH, ALU.mult, ALU.is_le).then_inc(flagged, 1)
                nc.vector.tensor_scalar(row[:, 4:5], row[:, 2:3], RMAX, None, ALU.is_le).then_inc(flagged, 1)
                dve.wait_ge(flagged, 4)
                nc.vector.tensor_tensor(S["flag"][0:1, 0:1], row[:, 3:4], row[:, 4:5], ALU.mult).then_inc(flagged, 1)
                dve.wait_ge(flagged, 5)

            @block.scalar
            def _(act):
                def batch(b, first):
                    layernorm_root(act, nc, st, ln, rooted, b * LN)
                    act.wait_ge(xn_turned, b + 1)
                    if not first:
                        act.wait_ge(qkv_made, 3 * b)
                    nc.scalar.activation(xnT[:, 0:1024], x_ps[:, 0:2, :].rearrange("p a n -> p (a n)"), ACT.Copy)
                    nc.scalar.activation(xnT[:, 1024:N], x_ps[:, 2, 0:P], ACT.Copy).then_inc(xnT_made, 1)
                    act.wait_ge(qkv_made, 3 * b + 1)
                    if not first:
                        act.wait_ge(stored, b * 16 * STORES)
                        act.wait_ge(ranged, 2 * b + 1)
                    nc.scalar.activation(qk[:, 0, :].rearrange("p (i n) -> p i n", i=NQ), q_ps[:, :, 0:QC], ACT.Copy).then_inc(q_out, 1)
                    act.wait_ge(qkv_made, 3 * b + 3)
                    act.wait_ge(ones_set, 1)
                    for i in range(NQ):
                        last = nc.scalar.activation(va[:, :, 3 * i:3 * i + 3, 0:DH],
                                                    q_ps[:, i, 0:QC].rearrange("p (t h d) -> p h t d", t=3, h=HEADS), ACT.Copy)
                    last.then_inc(v_out, 1)

                batch(0, True)
                with act.Fori(1, BATCH) as b:
                    batch(b, False)


def layernorm(dve, nc, x, xc, sq, st, done, rooted, at, round_):
    wide = lambda s: st[:, s, :].rearrange("p (t o) -> p t o", o=1).to_broadcast([P, KT, C])
    nc.vector.tensor_reduce(st[:, 0, :], x[:], AX.X, ALU.add).then_inc(done, 1)
    dve.wait_ge(done, at + 1)
    nc.vector.tensor_scalar(st[:, 1, :], st[:, 0, :], 1.0 / C, None, ALU.mult).then_inc(done, 1)
    dve.wait_ge(done, at + 2)
    nc.vector.tensor_tensor(xc[:], x[:], wide(1), ALU.subtract).then_inc(done, 1)
    dve.wait_ge(done, at + 3)
    nc.vector.tensor_tensor(sq[:], xc[:], xc[:], ALU.mult).then_inc(done, 1)
    dve.wait_ge(done, at + 4)
    nc.vector.tensor_reduce(st[:, 2, :], sq[:], AX.X, ALU.add).then_inc(done, 1)
    dve.wait_ge(done, at + 5)
    nc.vector.tensor_scalar(st[:, 3, :], st[:, 2, :], 1.0 / C, EPS_LN, ALU.mult, ALU.add).then_inc(done, 1)
    dve.wait_ge(rooted, round_ + 1)
    nc.vector.reciprocal(st[:, 5, :], st[:, 4, :]).then_inc(done, 1)
    dve.wait_ge(done, at + 7)
    nc.vector.tensor_tensor(st[:, 0, :], st[:, 5, :], st[:, 5, :], ALU.mult).then_inc(done, 1)
    dve.wait_ge(done, at + 8)
    nc.vector.tensor_tensor(st[:, 2, :], st[:, 0, :], st[:, 3, :], ALU.mult).then_inc(done, 1)
    dve.wait_ge(done, at + 9)
    nc.vector.tensor_scalar(st[:, 0, :], st[:, 2, :], -0.5, 1.5, ALU.mult, ALU.add).then_inc(done, 1)
    dve.wait_ge(done, at + 10)
    nc.vector.tensor_tensor(st[:, 1, :], st[:, 5, :], st[:, 0, :], ALU.mult).then_inc(done, 1)
    dve.wait_ge(done, at + 11)
    nc.vector.tensor_tensor(xc[:], xc[:], wide(1), ALU.mult).then_inc(done, 1)


def layernorm_root(act, nc, st, done, rooted, at):
    act.wait_ge(done, at + 6)
    nc.scalar.activation(st[:, 4, :], st[:, 3, :], ACT.Sqrt).then_inc(rooted, 1)


JOBS = {u: [("waves", u // 4, u % 4, i) for i in range(NQ)] for u in (0, 1, 2, 4, 5, 6)}
JOBS |= {u: [("exponent", u // 4, 0, i) for i in range(NQ)] for u in (3, 7)}
JOBS[8] = []
JPH = sum(map(len, JOBS.values()))
JOB_AT = {u: sum(len(JOBS[v]) for v in range(u)) for u in JOBS}
WAVES_DONE = [NT * NQ, NT * NQ + NQ + NT * NQ]
SIDE_DONE = [NT * NQ + NQ, JPH]
SINES = {(3, 0): 0, (7, 0): 1}
SPLITS = {(3, 1): (0, 0), (3, 2): (0, 1), (4, 1): (0, 2), (7, 0): (1, 0), (7, 1): (1, 1), (7, 2): (1, 2)}
CHAIN = [p for p in GPOS if p != 0]
DVE_PER_UNIT = len(CHAIN)
STEP = 2 * UNITS
JOB_SLOTS = (0, 3, 6)
POWER_STEPS = {0: (0, (0, 1)), 1: (0, (2, 3, 4)), 4: (1, (0, 1)), 5: (1, (2, 3, 4))}
POOL_STEPS = {1: (0, (0, 1, 2)), 2: (0, (3, 4)), 5: (1, (0, 1, 2)), 6: (1, (3, 4))}
SCALED = 9
GNORM = 1.0 / (GSCALE ** 2 * WAVES)
SPREADS = [sum(3 * min(TP, PAIRS - TP * t) for side in range(2) for t in range(NT) if (NT * side + t) % 2 == stage)
           for stage in range(2)]


def spreads_before(h, side, t):
    stage = (NT * side + t) % 2
    return SPREADS[stage] * h + sum(3 * min(TP, PAIRS - TP * b) for a in range(2) for b in range(NT)
                                    if NT * a + b < NT * side + t and (NT * a + b) % 2 == stage)


def at_parity(u, n):
    return (JOB_AT[u] + n) % 2


def fast_attention(nc, A, S):
    with ExitStack() as ctx:
        sb = lambda name, shape, dt=F32: ctx.enter_context(nc.sbuf_tensor(name, shape, dt))
        sem = lambda name: ctx.enter_context(nc.semaphore(name))
        wq = sb("f_wq", [AROWS, 2, PAIRS, N], F16)
        wk = sb("f_wk", [AROWS, 2, PAIRS, N], F16)
        ex = sb("f_ex", [LROWS, 2, 2, 2, N], F16)
        vv = sb("f_vv", [P, 2, KT, VW])
        xs = sb("f_xs", [PROWS, N])
        x2 = sb("f_x2", [PROWS, N])
        x4 = sb("f_x4", [PROWS, N])
        xb = sb("f_xb", [PROWS, N])
        pw = sb("f_pw", [PROWS, POWERS // PB, N])
        rows = sb("f_rows", [KBASE + VW, N])
        near = sb("f_near", [AROWS, 2, QC])
        wave = sb("f_wave", [AROWS, NT, N])
        part = sb("f_part", [AROWS, 2, 2, N], F16)
        prod = sb("f_prod", [P, 2, KG, QC])
        expo = sb("f_expo", [P, 2, KG, QC])
        pow4 = sb("f_pow4", [P, 2, KG, QC])
        sums = sb("f_sums", [VW, 2, QC])
        angles = sb("f_angles", [KBASE + VW, NT, AROWS])
        project = sb("f_project", [PROWS, 2, POWERS // PB, LROWS])
        lift = sb("f_lift", [LROWS, 2])
        bits = sb("f_bits", [PROWS, 6])
        bits2 = sb("f_bits2", [PROWS, 1])
        r_ = sb("f_r", [P, 8])
        slots = ctx.enter_context(nc.psum_tensor("f_slots", [P, 2, KG, 512], F32))
        av_ps = ctx.enter_context(nc.psum_tensor("f_av_ps", [P, 512], F32))
        feat_ps = ctx.enter_context(nc.psum_tensor("f_feat_ps", [P, 512], F32))

        consts_in, scaled, ones_set = sem("f_consts_in"), sem("f_scaled"), sem("f_ones_set")
        x_in, rows_in = sem("f_x_in"), sem("f_rows_in")
        v_in = [sem("f_v_in0"), sem("f_v_in1")]
        out_stored = [sem("f_out_stored0"), sem("f_out_stored1")]
        spread = [sem("f_spread0"), sem("f_spread1")]
        filled, job_made, job_near, job_done = sem("f_filled"), sem("f_job_made"), sem("f_job_near"), sem("f_job_done")
        powers_a, powers_b, sined, high, rest = sem("f_powers_a"), sem("f_powers_b"), sem("f_sined"), sem("f_high"), sem("f_rest")
        seeded, exped, chained, squared, fourthed, weighed = (sem("f_seeded"), sem("f_exped"), sem("f_chained"),
                                                              sem("f_squared"), sem("f_fourthed"), sem("f_weighed"))
        summed, read_out = sem("f_summed"), sem("f_read_out")

        def unit(j, w):
            return STEP * j + w, w % UNITS, 2 * j + w // UNITS + 1

        def freed(eng, u, p, static_first):
            if p < 2:
                if static_first:
                    return
                u, p = u - 1, p + SLOTS
            p -= 2
            if p == 0:
                eng.wait_ge(seeded, u + 1)
            elif p == LPOS:
                eng.wait_ge(exped, u + 1)
            else:
                eng.wait_ge(chained, DVE_PER_UNIT * u + CHAIN.index(p) + 1)

        with nc.Block() as block:
            @block.sync
            def _(sp):
                flag = sp.value_load(S["flag"][0:1, 0:1], min_val=0, max_val=1)
                with sp.If(flag > 0):
                    for what, where in (("angles", angles), ("project", project), ("lift", lift), ("bits", bits)):
                        sp.dma_start(where[:], A[what]).then_inc(consts_in, 16)
                    sp.dma_start(r_[:, 0:1], A["R"].to_broadcast([P, 1])).then_inc(consts_in, 16)

                    def head_of(what, h):
                        return S[what].rearrange("b (h d) n -> (b h) d n", d=DH)[bass.ds(h, 1)].rearrange("o d n -> (o d) n")

                    def load_x(h, side):
                        sp.wait_ge(powers_b, 5 * (2 * h + side))
                        for b in range(PB):
                            sp.dma_start(xs[b * DH:(b + 1) * DH, :], head_of("qk"[side], h)).then_inc(x_in, 16)

                    def spread_side(h, par, side):
                        for t in range(NT):
                            stage = (NT * side + t) % 2
                            sp.wait_ge(rest, 2 * NT * h + NT * side + t + 1)
                            dst = (wq, wk)[side]
                            for pair in range(TP):
                                for place, which in enumerate(((0, 1, 0), (0, 0, 1))[side]):
                                    if TP * t + pair < PAIRS:
                                        sp.dma_start(dst[place * PF:(place + 1) * PF, par, TP * t + pair, :],
                                                     part[pair * PF:(pair + 1) * PF, stage, which, :]).then_inc(spread[stage], 16)

                    def features(h, par, first, stores):
                        load_x(h, 0)
                        sp.wait_ge(job_made, JPH * h)
                        sp.wait_ge(ones_set, 1)
                        for side in range(2):
                            if side and not first:
                                sp.wait_ge(filled, SLOTS * UNITS * (h - 1))
                            sp.dma_start(rows[KBASE * side:KBASE * side + DH, :], head_of("qk"[side], h)).then_inc(rows_in, 16)
                        if not first:
                            sp.wait_ge(weighed, UNITS * (h - 1))
                        sp.dma_start(vv[:, par], S["v"].rearrange("b h p t v -> (b h) p t v")[bass.ds(h, 1)]
                                     .rearrange("o p t v -> (o p) t v")).then_inc(v_in[par], 16)
                        stores(0)
                        load_x(h, 1)
                        spread_side(h, par, 0)
                        stores(1)
                        spread_side(h, par, 1)
                        stores(2)

                    def head(n, hh, first):
                        def stores(k):
                            if k > 0 or not first:
                                out_group(n, hh, k - 1)
                        features(n + 1, (hh + 1) % 2, False, stores)

                    def out_group(n, hh, i):
                        h, place = (n, i) if i >= 0 else (n - 1, NQ - 1)
                        ring = (NQ * hh + i) % 2
                        sp.wait_ge(read_out, NQ * n + i + 1)
                        sp.dma_start(S["out"].rearrange("b h v n -> (b h) v n")[bass.ds(h, 1)].rearrange("o v n -> (o v) n")
                                     [:, place * QC:(place + 1) * QC], sums[:, ring, :]).then_inc(out_stored[ring], 16)

                    features(0, 0, True, lambda k: None)
                    head(0, 0, True)
                    head(1, 1, False)
                    with sp.Fori(1, BH // 2) as j:
                        head(2 * j, 0, False)
                        head(2 * j + 1, 1, False)
                    out_group(BH, 0, -1)
                    for ring in range(2):
                        sp.wait_ge(out_stored[ring], 16 * NQ * BH // 2)
                    for stage in range(2):
                        sp.wait_ge(spread[stage], 16 * SPREADS[stage] * (BH + 1))
                    sp.wait_ge(v_in[0], 16 * (BH // 2 + 1))

            @block.tensor
            def _(pe):
                flag = pe.value_load(S["flag"][0:1, 0:1], min_val=0, max_val=1)
                with pe.If(flag > 0):
                    def job(h, par, u, n):
                        kind, side, t, i = JOBS[u][n]
                        at = JPH * h + JOB_AT[u] + n
                        if type(at) is not int or at > 0:
                            pe.wait_ge(job_done, at)
                        if kind == "waves":
                            pe.wait_ge(rows_in, 32 * (h + 1))
                            base = KBASE * side
                            mm = nc.tensor.matmul(feat_ps[0:AROWS, 0:QC], angles[base:base + VW, t, :],
                                                  rows[base:base + VW, i * QC:(i + 1) * QC], start=True, stop=True)
                        else:
                            pe.wait_ge(powers_b, 5 * (2 * h + side) + 5)
                            for k in range(POWERS // PB):
                                mm = nc.tensor.matmul(feat_ps[0:LROWS, 0:QC], project[:, side, k, :],
                                                      pw[:, k, i * QC:(i + 1) * QC], start=(k == 0), stop=(k == POWERS // PB - 1))
                        mm.then_inc(job_made, 1)

                    def fill(u, w, p, par, static_first):
                        freed(pe, u, p, static_first)
                        qc, kg = w % UNITS // KG, w % KG
                        q = slice(qc * QC, (qc + 1) * QC)
                        slot = (SLOTS * w + p) % 2
                        for k in range(KG):
                            kt = slice((kg * KG + k) * P, (kg * KG + k + 1) * P)
                            if p == LPOS:
                                for n, (a, b) in enumerate(((0, 0), (1, 0), (0, 1))):
                                    mm = nc.tensor.matmul(slots[:, slot, k, 0:QC], ex[:, par, 1, b, kt], ex[:, par, 0, a, q],
                                                          start=(n == 0), stop=(n == 2))
                            else:
                                pair = GPOS.index(p)
                                mm = nc.tensor.matmul(slots[:, slot, k, 0:QC], wk[:, par, pair, kt], wq[:, par, pair, q],
                                                      start=True, stop=True)
                        mm.then_inc(filled, 1)

                    def weigh(j, w):
                        kg, par = w % KG, w % STEP // UNITS
                        pe.wait_ge(fourthed, STEP * j + w + 1)
                        if kg == 0 and not (type(j) is int and j == 0 and w == 0):
                            pe.wait_ge(read_out, STEP // KG * j + w // KG)
                        for k in range(KG):
                            mm = nc.tensor.matmul(av_ps[0:VW, 0:QC], vv[:, par, kg * KG + k, :], pow4[:, w % 2, k, :],
                                                  start=(kg == 0 and k == 0), stop=(kg == KG - 1 and k == KG - 1))
                        mm.then_inc(weighed, 1)

                    pe.wait_ge(consts_in, 16 * 5)
                    pe.wait_ge(scaled, SCALED)
                    for u in range(UNITS):
                        for n in range(len(JOBS[u])):
                            job(0, 0, u, n)

                    def step(j, first):
                        for w in range(2 * UNITS):
                            u, v, h = unit(j, w)
                            par = w // UNITS
                            if v == 0:
                                for stage in range(2):
                                    pe.wait_ge(spread[stage], 16 * SPREADS[stage] * h)
                                pe.wait_ge(job_done, JPH * h)
                                pe.wait_ge(v_in[par], 16 * (j + 1))
                            for p in range(SLOTS):
                                fill(u, w, p, par, first and w == 0)
                                if p in JOB_SLOTS and JOB_SLOTS.index(p) < len(JOBS[v]):
                                    job(h, 1 - par, v, JOB_SLOTS.index(p))
                            if not (first and w == 0):
                                weigh(j, w - 1)

                    step(0, True)
                    with pe.Fori(1, BH // 2) as j:
                        step(j, False)
                    weigh(BH // 2, -1)

            @block.scalar
            def _(act):
                flag = act.value_load(S["flag"][0:1, 0:1], min_val=0, max_val=1)
                with act.If(flag > 0):
                    def job(h, par, u, n):
                        kind, side, t, i = JOBS[u][n]
                        at = JPH * h + JOB_AT[u] + n
                        act.wait_ge(job_made, at + 1)
                        if kind == "waves":
                            if not (type(at) is int and at < 2):
                                act.wait_ge(job_done, at - 1)
                            nc.scalar.activation(near[:, at_parity(u, n), :], feat_ps[0:AROWS, 0:QC], ACT.Identity,
                                                 bias=r_[0:AROWS, 4:5]).then_inc(job_near, 1)
                        else:
                            nc.scalar.activation(ex[:, par, side, 0, i * QC:(i + 1) * QC], feat_ps[0:LROWS, 0:QC], ACT.Identity,
                                                 bias=lift[:, side:side + 1]).then_inc(job_near, 1)

                    def power(h, side, n):
                        at = 5 * (2 * h + side)
                        if n == 0:
                            act.wait_ge(x_in, 16 * PB * (2 * h + side + 1))
                            act.wait_ge(powers_b, at)
                            nc.scalar.activation(x2[:], xs[:], ACT.Square, scale=r_[0:PROWS, 1:2]).then_inc(powers_a, 1)
                        elif n == 1:
                            act.wait_ge(job_made, JPH * h + (SIDE_DONE[0] if side else 0))
                            nc.scalar.activation(pw[:, 0, :], xs[:], ACT.Identity, scale=bits2[:, 0:1], bias=bits[:, 3:4]).then_inc(powers_a, 1)
                        elif n == 2:
                            act.wait_ge(powers_a, at + 1)
                            nc.scalar.activation(x4[:], x2[:], ACT.Square).then_inc(powers_a, 1)
                        elif n == 3:
                            nc.scalar.activation(xb[:], x2[:], ACT.Identity, scale=bits[:, 1:2], bias=bits[:, 4:5]).then_inc(powers_a, 1)
                        else:
                            act.wait_ge(powers_a, at + 3)
                            nc.scalar.activation(xs[:], x4[:], ACT.Identity, scale=bits[:, 2:3], bias=bits[:, 5:6]).then_inc(powers_a, 1)

                    def sines(h, side):
                        act.wait_ge(job_done, JPH * h + WAVES_DONE[side])
                        for t in range(NT):
                            nc.scalar.activation(wave[:, t, :], wave[:, t, :], ACT.Sin, scale=2 * pi).then_inc(sined, 1)

                    def split_high(h, side, t):
                        stage = (NT * side + t) % 2
                        act.wait_ge(sined, 2 * NT * h + NT * side + t + 1)
                        if not (type(h) is int and h == 0 and NT * side + t < 2):
                            act.wait_ge(spread[stage], 16 * spreads_before(h, side, t))
                        nc.scalar.activation(part[:, stage, 0, :], wave[:, t, :], ACT.Copy, scale=GSCALE).then_inc(high, 1)

                    def features(h, par, v, n):
                        if (v, n) in SINES:
                            sines(h, SINES[v, n])
                        if (v, n) in SPLITS:
                            split_high(h, *SPLITS[v, n])
                        if n == 1 and v in POWER_STEPS:
                            side, steps = POWER_STEPS[v]
                            for k in steps:
                                power(h, side, k)
                        if n < len(JOBS[v]):
                            job(h, par, v, n)

                    def square(u, w):
                        act.wait_ge(chained, DVE_PER_UNIT * (u + 1))
                        if not (type(u) is int and u < 2):
                            act.wait_ge(weighed, u - 1)
                        nc.scalar.activation(pow4[:, w % 2], prod[:, w % 2], ACT.Square, scale=r_[:, 3:4]).then_inc(squared, 1)

                    def square_again(u, w):
                        act.wait_ge(squared, 2 * u + 1)
                        nc.scalar.activation(pow4[:, w % 2], pow4[:, w % 2], ACT.Square).then_inc(squared, 1)

                    def read_sums(j, w):
                        ring = w // KG % 2
                        act.wait_ge(weighed, STEP * j + w + 1)
                        if not (type(j) is int and j == 0 and w < 2 * KG):
                            act.wait_ge(out_stored[ring], 16 * (STEP // KG // 2 * j + w // KG // 2))
                        nc.scalar.activation(sums[:, ring, :], av_ps[0:VW, 0:QC], ACT.Copy).then_inc(read_out, 1)

                    act.wait_ge(consts_in, 16 * 5)
                    act.wait_ge(scaled, SCALED)
                    for v in range(UNITS):
                        for n in range(3):
                            features(0, 0, v, n)

                    def step(j, first):
                        for w in range(2 * UNITS):
                            u, v, h = unit(j, w)
                            par = w // UNITS
                            before = w - 1 if w else 2 * UNITS - 1
                            start = first and w == 0
                            act.wait_ge(filled, SLOTS * u + 1)
                            if not (first and w < 2):
                                act.wait_ge(squared, 2 * (u - 2) + 1)
                            nc.scalar.activation(prod[:, w % 2], slots[:, SLOTS * w % 2, :, 0:QC], ACT.Copy, scale=GNORM).then_inc(seeded, 1)
                            features(h, 1 - par, v, 0)
                            if not start:
                                square(u - 1, before)
                            features(h, 1 - par, v, 1)
                            act.wait_ge(filled, SLOTS * u + LPOS + 1)
                            if not (first and w < 2):
                                act.wait_ge(fourthed, u - 1)
                            nc.scalar.activation(expo[:, w % 2], slots[:, (SLOTS * w + LPOS) % 2, :, 0:QC], ACT.Exp,
                                                 scale=1.0 / LSCALE ** 2).then_inc(exped, 1)
                            if not start:
                                square_again(u - 1, before)
                            features(h, 1 - par, v, 2)
                            if v % KG == 1 and not (first and w < KG):
                                read_sums(j, w - 2)

                    step(0, True)
                    with act.Fori(1, BH // 2) as j:
                        step(j, False)
                    square(UNITS * BH - 1, 2 * UNITS - 1)
                    square_again(UNITS * BH - 1, 2 * UNITS - 1)
                    read_sums(BH // 2, -1)

            @block.vector
            def _(dve):
                flag = dve.value_load(S["flag"][0:1, 0:1], min_val=0, max_val=1)
                with dve.If(flag > 0):
                    dve.memset(rows[:], 1.0).then_inc(ones_set, 1)
                    dve.memset(r_[:, 4:5], MAGIC).then_inc(scaled, 1)
                    dve.wait_ge(consts_in, 16 * 5)
                    nc.vector.tensor_scalar(r_[:, 1:2], r_[:, 0:1], 1.0 / REACH, None, ALU.mult).then_inc(scaled, 1)
                    for i, (a, b) in enumerate(((0, 2), (2, 5), (5, 6), (6, 3))):
                        nc.vector.tensor_scalar(r_[:, b:b + 1], r_[:, a:a + 1], r_[:, a:a + 1], None, ALU.mult).then_inc(scaled, 1)
                        dve.wait_ge(scaled, i + 3)
                    nc.vector.tensor_scalar(bits2[:, 0:1], bits[:, 0:1], r_[0:PROWS, 1:2], None, ALU.mult).then_inc(scaled, 1)
                    for base in (0, KBASE):
                        part_ = angles[base:base + DH].rearrange("r t c -> r (t c)")
                        nc.vector.tensor_scalar(part_, part_, r_[base:base + DH, 0:1], None, ALU.mult).then_inc(scaled, 1)

                    def job(h, par, u, n):
                        kind, side, t, i = JOBS[u][n]
                        at = JPH * h + JOB_AT[u] + n
                        dve.wait_ge(job_near, at + 1)
                        if kind == "waves":
                            nc.vector.scalar_tensor_tensor(wave[:, t, i * QC:(i + 1) * QC], near[:, at_parity(u, n), :], MAGIC,
                                                           feat_ps[0:AROWS, 0:QC], ALU.subtract, ALU.subtract).then_inc(job_done, 1)
                        else:
                            nc.vector.scalar_tensor_tensor(ex[:, par, side, 1, i * QC:(i + 1) * QC], feat_ps[0:LROWS, 0:QC],
                                                           lift[:, side:side + 1], ex[:, par, side, 0, i * QC:(i + 1) * QC],
                                                           ALU.add, ALU.subtract).then_inc(job_done, 1)

                    def split_rest(h, side, t):
                        dve.wait_ge(high, 2 * NT * h + NT * side + t + 1)
                        stage = (NT * side + t) % 2
                        nc.vector.scalar_tensor_tensor(part[:, stage, 1, :], wave[:, t, :], GSCALE, part[:, stage, 0, :],
                                                       ALU.mult, ALU.subtract).then_inc(rest, 1)

                    def features(h, par, v, n):
                        if n < len(JOBS[v]):
                            job(h, par, v, n)
                        if (v, n) in SPLITS:
                            split_rest(h, *SPLITS[v, n])

                    for v in range(UNITS):
                        for n in range(3):
                            features(0, 0, v, n)

                    def step(j, first):
                        for w in range(2 * UNITS):
                            u, v, h = unit(j, w)
                            for c, p in enumerate(CHAIN):
                                if c == 0:
                                    dve.wait_ge(seeded, u + 1)
                                else:
                                    dve.wait_ge(chained, DVE_PER_UNIT * u + c)
                                dve.wait_ge(filled, SLOTS * u + p + 1)
                                nc.vector.scalar_tensor_tensor(prod[:, w % 2], slots[:, (SLOTS * w + p) % 2, :, 0:QC], GNORM,
                                                               prod[:, w % 2], ALU.mult, ALU.mult).then_inc(chained, 1)
                                if c in (1, 3, 5):
                                    features(h, 1 - w // UNITS, v, c // 2)

                    step(0, True)
                    with dve.Fori(1, BH // 2) as j:
                        step(j, False)

            @block.gpsimd
            def _(pool):
                flag = pool.value_load(S["flag"][0:1, 0:1], min_val=0, max_val=1)
                with pool.If(flag > 0):
                    def power(h, side, n):
                        at = 5 * (2 * h + side)
                        if n == 0:
                            pool.wait_ge(powers_a, at + 4)
                            nc.gpsimd.tensor_tensor(pw[:, 0, :], pw[:, 0, :], xb[:], ALU.mult).then_inc(powers_b, 1)
                        elif n == 1:
                            pool.wait_ge(powers_a, at + 5)
                            pool.wait_ge(powers_b, at + 1)
                            nc.gpsimd.tensor_tensor(pw[:, 0, :], pw[:, 0, :], xs[:], ALU.mult).then_inc(powers_b, 1)
                        elif n == 2:
                            nc.gpsimd.tensor_tensor(x2[:], x2[:], x4[:], ALU.mult).then_inc(powers_b, 1)
                        else:
                            pool.wait_ge(powers_b, at + n)
                            nc.gpsimd.tensor_tensor(pw[:, n - 2, :], pw[:, n - 3, :], x2[:], ALU.mult).then_inc(powers_b, 1)

                    def features(h, v):
                        if v in POOL_STEPS:
                            side, steps = POOL_STEPS[v]
                            for k in steps:
                                power(h, side, k)

                    for v in range(UNITS):
                        features(0, v)

                    def step(j):
                        for w in range(2 * UNITS):
                            u, v, h = unit(j, w)
                            features(h, v)
                            pool.wait_ge(squared, 2 * u + 2)
                            pool.wait_ge(exped, u + 1)
                            nc.gpsimd.tensor_tensor(pow4[:, w % 2], pow4[:, w % 2], expo[:, w % 2], ALU.mult).then_inc(fourthed, 1)

                    step(0)
                    with pool.Fori(1, BH // 2) as j:
                        step(j)


def general_attention(nc, A, S):
    with ExitStack() as ctx:
        sb = lambda name, shape, dt=F32: ctx.enter_context(nc.sbuf_tensor(name, shape, dt))
        sem = lambda name: ctx.enter_context(nc.semaphore(name))
        q_all = sb("g_q", [P, DH, N])
        k_col = sb("g_k", [P, DH])
        v_col = sb("g_v", [P, VW])
        x, dist, turn, half, sine = (sb(f"g_{n}", [P, N]) for n in ("x", "dist", "turn", "half", "sine"))
        num, den, inv, score, weight = (sb(f"g_{n}", [P, N]) for n in ("num", "den", "inv", "score", "weight"))
        acc = sb("g_acc", [VW, N])
        r_ = sb("g_r", [P, 4])
        sums_ps = ctx.enter_context(nc.psum_tensor("g_sums", [P, NQ, 512], F32))
        r_in, r_made, q_in, kv_in = sem("g_r_in"), sem("g_r_made"), sem("g_q_in"), sem("g_kv_in")
        fun, summed, added, cleared, stored = (sem(f"g_{n}") for n in ("fun", "summed", "added", "cleared", "stored"))
        vec = [sem(f"g_vec{n}") for n in range(4)]
        VEC, FUN = 4 * 7 + 3, 2 * DH + 2

        with nc.Block() as block:
            @block.sync
            def _(sp):
                flag = sp.value_load(S["flag"][0:1, 0:1], min_val=0, max_val=1)
                with sp.If(flag < 1):
                    sp.dma_start(r_[:, 0:1], A["R"].to_broadcast([P, 1])).then_inc(r_in, 16)
                    heads = lambda what, h: S[what].rearrange("b (h d) n -> (b h) d n", d=DH)[bass.ds(h, 1)]
                    with sp.Fori(0, BH) as h:
                        sp.wait_ge(vec[3], h * (KT * VEC))
                        sp.dma_start(q_all[:], heads("q", h).to_broadcast([P, DH, N])).then_inc(q_in, 16)
                        with sp.Fori(0, KT) as t:
                            sp.wait_ge(summed, h * KT + t)
                            with nc.allow_non_contiguous_dma(reason="keys by rows"):
                                sp.dma_start(k_col[:], heads("k", h).rearrange("o d n -> (o n) d")[bass.ds(t * P, P), :]).then_inc(kv_in, 16)
                            sp.dma_start(v_col[:], S["v"].rearrange("b h p t v -> (b h) t p v")[bass.ds(h, 1), bass.ds(t, 1)]
                                         .rearrange("o t p v -> (o t p) v")).then_inc(kv_in, 16)
                        sp.wait_ge(added, (h + 1) * KT)
                        sp.dma_start(S["out"].rearrange("b h v n -> (b h) v n")[bass.ds(h, 1)].rearrange("o v n -> (o v) n"),
                                     acc[:]).then_inc(stored, 16)
                    sp.wait_ge(stored, 16 * BH)

            @block.vector
            def _(dve):
                flag = dve.value_load(S["flag"][0:1, 0:1], min_val=0, max_val=1)
                with dve.If(flag < 1):
                    dve.memset(r_[:, 3:4], MAGIC).then_inc(r_made, 1)
                    dve.wait_ge(r_in, 16)
                    nc.vector.scalar_tensor_tensor(r_[:, 1:2], r_[:, 0:1], -1.0, r_[:, 0:1], ALU.mult, ALU.max).then_inc(r_made, 1)
                    dve.wait_ge(r_made, 2)
                    nc.vector.tensor_scalar(r_[:, 2:3], r_[:, 1:2], 1.0 / pi, None, ALU.mult).then_inc(r_made, 1)
                    dve.wait_ge(r_made, 3)
                    with dve.Fori(0, BH) as h:
                        dve.wait_ge(stored, 16 * h)
                        nc.vector.memset(acc[:], 0.0).then_inc(cleared, 1)
                        with dve.Fori(0, KT) as t:
                            m = h * KT + t
                            dve.wait_ge(cleared, h + 1)
                            dve.wait_ge(q_in, 16 * (h + 1))
                            dve.wait_ge(kv_in, 32 * (m + 1))
                            for d in range(DH):
                                step = vec[d // 4]
                                at, fat = m * VEC + 7 * (d % 4), m * FUN + 2 * d
                                nc.vector.tensor_scalar(x[:], q_all[:, d, :], k_col[:, d:d + 1], None, ALU.subtract).then_inc(step, 1)
                                dve.wait_ge(step, at + 1)
                                nc.vector.scalar_tensor_tensor(dist[:], x[:], -1.0, x[:], ALU.mult, ALU.max).then_inc(step, 1)
                                dve.wait_ge(step, at + 2)
                                nc.vector.tensor_scalar(dist[:], dist[:], NEAR, None, ALU.max).then_inc(step, 1)
                                dve.wait_ge(fun, fat + 1)
                                nc.vector.tensor_scalar(turn[:], turn[:], MAGIC, None, ALU.subtract).then_inc(step, 1)
                                dve.wait_ge(step, at + 4)
                                nc.vector.scalar_tensor_tensor(half[:], dist[:], r_[:, 2:3], turn[:], ALU.mult, ALU.subtract).then_inc(step, 1)
                                dve.wait_ge(fun, fat + 2)
                                if d % 4 == 0:
                                    nc.vector.tensor_copy(num[:], sine[:]).then_inc(step, 1)
                                    nc.vector.tensor_copy(den[:], dist[:]).then_inc(step, 1)
                                else:
                                    nc.vector.tensor_tensor(num[:], num[:], sine[:], ALU.mult).then_inc(step, 1)
                                    nc.vector.tensor_tensor(den[:], den[:], dist[:], ALU.mult).then_inc(step, 1)
                                if d % 4 == 3:
                                    dve.wait_ge(step, at + 7)
                                    nc.vector.reciprocal(inv[:], den[:]).then_inc(step, 1)
                                    dve.wait_ge(step, at + 8)
                                    nc.vector.tensor_tensor(inv[:], inv[:], num[:], ALU.mult).then_inc(step, 1)
                                    dve.wait_ge(step, at + 9)
                                    if d == 3:
                                        nc.vector.tensor_copy(score[:], inv[:]).then_inc(step, 1)
                                    else:
                                        nc.vector.tensor_tensor(score[:], score[:], inv[:], ALU.mult).then_inc(step, 1)
                                dve.wait_ge(step, at + (10 if d % 4 == 3 else 7))
                            dve.wait_ge(summed, m + 1)
                            nc.vector.tensor_tensor(acc[:].rearrange("v (i n) -> v i n", i=NQ), acc[:].rearrange("v (i n) -> v i n", i=NQ),
                                                    sums_ps[0:VW, :, 0:QC], ALU.add).then_inc(added, 1)
                            dve.wait_ge(added, m + 1)

            @block.scalar
            def _(act):
                flag = act.value_load(S["flag"][0:1, 0:1], min_val=0, max_val=1)
                with act.If(flag < 1):
                    act.wait_ge(r_made, 3)
                    with act.Fori(0, BH) as h:
                        with act.Fori(0, KT) as t:
                            m = h * KT + t
                            for d in range(DH):
                                act.wait_ge(vec[d // 4], m * VEC + 7 * (d % 4) + 3)
                                nc.scalar.activation(turn[:], dist[:], ACT.Identity, scale=r_[:, 2:3], bias=r_[:, 3:4]).then_inc(fun, 1)
                                act.wait_ge(vec[d // 4], m * VEC + 7 * (d % 4) + 5)
                                nc.scalar.activation(sine[:], half[:], ACT.Sin, scale=pi).then_inc(fun, 1)
                            act.wait_ge(vec[3], (m + 1) * VEC)
                            act.wait_ge(summed, m)
                            nc.scalar.activation(weight[:], score[:], ACT.Square).then_inc(fun, 1)
                            act.wait_ge(fun, m * FUN + 2 * DH + 1)
                            nc.scalar.activation(weight[:], weight[:], ACT.Square).then_inc(fun, 1)

            @block.tensor
            def _(pe):
                flag = pe.value_load(S["flag"][0:1, 0:1], min_val=0, max_val=1)
                with pe.If(flag < 1):
                    with pe.Fori(0, BH) as h:
                        with pe.Fori(0, KT) as t:
                            m = h * KT + t
                            pe.wait_ge(fun, (m + 1) * FUN)
                            pe.wait_ge(kv_in, 32 * (m + 1))
                            pe.wait_ge(added, m)
                            for i in range(NQ):
                                mm = nc.tensor.matmul(sums_ps[0:VW, i, 0:QC], v_col[:], weight[:, i * QC:(i + 1) * QC],
                                                      start=True, stop=True)
                            mm.then_inc(summed, 1)


def project_and_ffn(nc, A, S, out):
    with ExitStack() as ctx:
        sb = lambda name, shape, dt=F32: ctx.enter_context(nc.sbuf_tensor(name, shape, dt))
        sem = lambda name: ctx.enter_context(nc.semaphore(name))
        psum = lambda name, shape: ctx.enter_context(nc.psum_tensor(name, shape, F32))
        wproj, wattn, wnext = sb("c_wproj", [P, C]), sb("c_wattn", [P, C]), sb("c_wnext", [P, C])
        rows = sb("c_rows", [1, 3, C])
        cols = sb("c_cols", [P, 3])
        b1, b2 = sb("c_b1", [P, EXPERTS, HID // P]), sb("c_b2", [P, EXPERTS])
        w1, w2 = sb("c_w1", [P, EXPERTS, HID]), sb("c_w2", [P, EXPERTS, HID // P, C])
        ident, heads = sb("c_ident", [P, P]), sb("c_heads", [HEADS, P])
        raw, total, inv = sb("c_raw", [P, N]), sb("c_total", [HEADS, N]), sb("c_inv", [HEADS, N])
        att = sb("c_att", [P, N])
        h = sb("c_h", [P, KT, C])
        x1, x2, sq = sb("c_x1", [P, KT, C]), sb("c_x2", [P, KT, C]), sb("c_sq", [P, KT, C])
        st = sb("c_stat", [P, 6, KT])
        xfT, normT, xaT = sb("c_xfT", [P, N]), sb("c_normT", [P, N]), sb("c_xaT", [P, N])
        hid = sb("c_hid", [P, HID // P, N])
        yT = sb("c_yT", [P, N])
        fin = sb("c_fin", [P, KT, C])
        a_ps, b_ps = psum("c_a", [P, NQ, 512]), psum("c_b", [P, NQ, 512])
        g_ps = psum("c_g", [P, 2, 512])
        consts_in, sums_in, h_in, stored = sem("c_consts_in"), sem("c_sums_in"), sem("c_h_in"), sem("c_stored")
        mm, vec, fun, ln, rooted, hidden, gelued = (sem(f"c_{n}") for n in ("mm", "vec", "fun", "ln", "rooted", "hidden", "gelued"))
        ones_ready, eps_added = sem("c_ones_ready"), sem("c_eps_added")
        a9 = a_ps[:].rearrange("p a n -> p (a n)")[:, 0:N].rearrange("p (t c) -> p t c", c=C)
        b9 = b_ps[:].rearrange("p a n -> p (a n)")[:, 0:N].rearrange("p (t c) -> p t c", c=C)
        a3, b3 = a_ps[:, :, 0:QC], b_ps[:, :, 0:QC]
        by3 = lambda t: t.rearrange("p (i n) -> p i n", i=NQ)
        MM, VEC, FUN = 7, 8, 2
        NH = SEG // 2
        JOBS_H = 2 * 2 * (HID // P)

        with nc.Block() as block:
            @block.sync
            def _(sp):
                for where, what in ((wproj[:], "wprojT"), (wattn[:], "wattnT"), (wnext[:], "wnextT"), (rows[:, 0, :], "b_proj"),
                                    (rows[:, 1, :], "next_b"), (cols[:, 0:1], "ln_g"), (cols[:, 1:2], "ln_b"), (cols[:, 2:3], "attn_b"),
                                    (b1[:], "fc1_b"), (b2[:], "fc2_b"), (w1[:], "fc1_wT"), (w2[:], "fc2_wT"), (ident[:], "ident"),
                                    (heads[:], "heads")):
                    sp.dma_start(where, A[what]).then_inc(consts_in, 16)
                with sp.Fori(0, BATCH) as b:
                    sp.wait_ge(vec, b * VEC)
                    sp.dma_start(h[:], S["h"][bass.ds(b, 1)].rearrange("o p t c -> (o p) t c")).then_inc(h_in, 16)
                    sums = S["out"][bass.ds(b, 1)]
                    for k in range(HEADS):
                        sp.dma_start(raw[k * DH:(k + 1) * DH, :], sums[:, k, 0:DH, :].rearrange("o v n -> (o v) n")).then_inc(sums_in, 16)
                    sp.dma_start(total[:], sums[:, :, DH, :].rearrange("o h n -> (o h) n")).then_inc(sums_in, 16)
                    sp.wait_ge(vec, b * VEC + VEC)
                    o = out[bass.ds(b, 1)].rearrange("o (t p) c -> p (o t) c", p=P)
                    sp.dma_start(o, fin[:]).then_inc(stored, 16)
                sp.wait_ge(stored, BATCH * 16)

            @block.tensor
            def _(pe):
                pe.wait_ge(consts_in, 14 * 16)
                pe.wait_ge(ones_ready, 1)

                def turn(src, dst):
                    for t in range(KT):
                        last = nc.tensor.transpose(dst[:, t, :], src[:, t, :], ident[:])
                    return last

                def batch(b, j):
                    pe.wait_ge(vec, b * VEC + 1)
                    for i in range(NQ):
                        last = nc.tensor.matmul(a3[:, i, :], heads[:], inv[:, i * QC:(i + 1) * QC], start=True, stop=True)
                    last.then_inc(mm, 1)
                    pe.wait_ge(vec, b * VEC + 2)
                    for t in range(KT):
                        nc.tensor.matmul(b9[:, t, :], att[:, t * P:(t + 1) * P], wproj[:], start=True, stop=False)
                        last = nc.tensor.matmul(b9[:, t, :], rows[:, 2, :], rows[:, 0, :], start=False, stop=True)
                    last.then_inc(mm, 1)
                    pe.wait_ge(ln, (2 * b + 1) * LN)
                    turn(x1, a9).then_inc(mm, 1)
                    pe.wait_ge(ln, (2 * b + 2) * LN)
                    turn(x2, b9).then_inc(mm, 1)
                    pe.wait_ge(fun, b * FUN + 1)
                    pe.wait_ge(vec, b * VEC + 4)
                    for i in range(NQ):
                        last = nc.tensor.matmul(a3[:, i, :], wattn[:], normT[:, i * QC:(i + 1) * QC], start=True, stop=True)
                    last.then_inc(mm, 1)
                    pe.wait_ge(vec, b * VEC + 5)
                    for e in range(2):
                        for half in range(2):
                            for c in range(HID // P):
                                n = (2 * e + half) * (HID // P) + c
                                lo = e * SEG + half * NH
                                if n >= 2:
                                    pe.wait_ge(gelued, b * JOBS_H + n - 1)
                                nc.tensor.matmul(g_ps[:, n % 2, 0:NH], w1[:, 2 * j + e, c * P:(c + 1) * P], xaT[:, lo:lo + NH],
                                                 start=True, stop=True).then_inc(hidden, 1)
                    pe.wait_ge(gelued, (b + 1) * JOBS_H)
                    for i in range(4):
                        for c in range(HID // P):
                            last = nc.tensor.matmul((a_ps, b_ps)[i // 2][:, i % 2, 0:NH], w2[:, 2 * j + i // 2, c, :], hid[:, c, i * NH:(i + 1) * NH],
                                                    start=(c == 0), stop=(c == HID // P - 1))
                    last.then_inc(mm, 1)
                    pe.wait_ge(vec, b * VEC + 7)
                    for t in range(KT):
                        nc.tensor.matmul(a9[:, t, :], yT[:, t * P:(t + 1) * P], wnext[:], start=True, stop=False)
                        last = nc.tensor.matmul(a9[:, t, :], rows[:, 2, :], rows[:, 1, :], start=False, stop=True)
                    last.then_inc(mm, 1)

                with pe.Fori(0, MICRO) as m:
                    for j in range(BATCH // MICRO):
                        batch(m * (BATCH // MICRO) + j, j)

            @block.vector
            def _(dve):
                dve.memset(rows[:, 2, :], 1.0).then_inc(ones_ready, 1)
                dve.wait_ge(consts_in, 14 * 16)

                def batch(b, j):
                    dve.wait_ge(sums_in, (b + 1) * 16 * (HEADS + 1))
                    nc.vector.tensor_scalar(total[:], total[:], EPS_ATT, None, ALU.add).then_inc(eps_added, 1)
                    dve.wait_ge(eps_added, b + 1)
                    nc.vector.reciprocal(inv[:], total[:]).then_inc(vec, 1)
                    dve.wait_ge(mm, b * MM + 1)
                    nc.vector.tensor_tensor(by3(att[:]), by3(raw[:]), a3, ALU.mult).then_inc(vec, 1)
                    dve.wait_ge(mm, b * MM + 2)
                    dve.wait_ge(h_in, (b + 1) * 16)
                    nc.vector.tensor_tensor(h[:], h[:], b9, ALU.add).then_inc(vec, 1)
                    dve.wait_ge(vec, b * VEC + 3)
                    layernorm(dve, nc, h, x1, sq, st, ln, rooted, 2 * b * LN, 2 * b)
                    dve.wait_ge(ln, (2 * b + 1) * LN)
                    layernorm(dve, nc, x1, x2, sq, st, ln, rooted, (2 * b + 1) * LN, 2 * b + 1)
                    dve.wait_ge(mm, b * MM + 3)
                    nc.vector.tensor_copy(xfT[:].rearrange("p (t c) -> p t c", c=C), a9).then_inc(vec, 1)
                    dve.wait_ge(vec, b * VEC + 4)
                    dve.wait_ge(mm, b * MM + 5)
                    nc.vector.scalar_tensor_tensor(by3(xaT[:]), a3, cols[:, 2:3], by3(xfT[:]), ALU.add, ALU.add).then_inc(vec, 1)
                    dve.wait_ge(mm, b * MM + 6)
                    for e in range(2):
                        nc.vector.tensor_scalar(yT[:, e * SEG:(e + 1) * SEG].rearrange("p (i n) -> p i n", i=2), (a_ps, b_ps)[e][:, 0:2, 0:NH],
                                                b2[:, 2 * j + e:2 * j + e + 1], None, ALU.add).then_inc(vec, 1)
                    dve.wait_ge(fun, b * FUN + 2)
                    nc.vector.tensor_tensor(fin[:], fin[:], h[:], ALU.add).then_inc(vec, 1)

                with dve.Fori(0, MICRO) as m:
                    for j in range(BATCH // MICRO):
                        batch(m * (BATCH // MICRO) + j, j)

            @block.scalar
            def _(act):
                act.wait_ge(consts_in, 14 * 16)

                def batch(b, j):
                    layernorm_root(act, nc, st, ln, rooted, 2 * b * LN)
                    layernorm_root(act, nc, st, ln, rooted, (2 * b + 1) * LN)
                    act.wait_ge(mm, b * MM + 4)
                    nc.scalar.activation(normT[:].rearrange("p (t c) -> p t c", c=C), b9, ACT.Identity, scale=cols[:, 0:1],
                                         bias=cols[:, 1:2]).then_inc(fun, 1)
                    for n in range(JOBS_H):
                        e, half, c = n // (2 * (HID // P)), n // (HID // P) % 2, n % (HID // P)
                        lo = e * SEG + half * NH
                        act.wait_ge(hidden, b * JOBS_H + n + 1)
                        nc.scalar.activation(hid[:, c, lo:lo + NH], g_ps[:, n % 2, 0:NH], ACT.Gelu,
                                             bias=b1[:, 2 * j + e, c:c + 1]).then_inc(gelued, 1)
                    act.wait_ge(mm, b * MM + 7)
                    act.wait_ge(stored, b * 16)
                    nc.scalar.activation(fin[:], a9, ACT.Gelu).then_inc(fun, 1)

                with act.Fori(0, MICRO) as m:
                    for j in range(BATCH // MICRO):
                        batch(m * (BATCH // MICRO) + j, j)


def build(nc, A, out):
    internal = lambda name, shape: nc.dram_tensor(name, shape, F32, kind="Internal").ap()
    S = {
        "q": internal("s_q", (BATCH + 1, P, N)), "k": internal("s_k", (BATCH + 1, P, N)),
        "v": internal("s_v", (BATCH + 1, HEADS, P, KT, VW)), "h": internal("s_h", (BATCH, P, KT, C)),
        "out": internal("s_out", (BATCH, HEADS, VW, N)),
    }
    with nc.sbuf_tensor("flag", [1, 1], I32) as flag:
        S["flag"] = flag
        tokens_and_qkv(nc, A, S)
        fast_attention(nc, A, S)
        general_attention(nc, A, S)
    project_and_ffn(nc, A, S, out)


def kernel(**inputs):
    import concourse.bacc as bacc
    import numpy as np
    from concourse import mybir
    from concourse.bass_utils import run_bass_kernel_spmd

    a = {k: np.asarray(v) for k, v in inputs.items()}
    turn = lambda x, *axes: np.ascontiguousarray(np.transpose(x, axes))
    f = "L0_ffn_"
    col = lambda x: np.ascontiguousarray(x.reshape(C, 1))
    arrays = {
        "xT": turn(a["x"].reshape(BATCH, IMG, FEAT), 0, 2, 1), "txt": a["txt"], "tok_w": a["L0_tok_W"],
        "wqkvT": turn(a["L0_attn_w_qkv"], 1, 0), "R": a["L0_attn_paramR"].reshape(1, 1),
        "wprojT": turn(a["L0_attn_w_proj"], 1, 0), "b_proj": a["L0_attn_b_proj"].reshape(1, C),
        "ln_g": col(a[f + "ln_g"]), "ln_b": col(a[f + "ln_b"]), "attn_b": col(a[f + "attn_b"]),
        "wattnT": turn(a[f + "attn_w"], 1, 0), "wnextT": turn(a[f + "next_w"], 1, 0), "next_b": a[f + "next_b"].reshape(1, C),
        "fc1_wT": turn(a[f + "fc1_w"], 2, 0, 1), "fc1_b": turn(a[f + "fc1_b"].reshape(EXPERTS, HID // P, P), 2, 0, 1),
        "fc2_wT": turn(a[f + "fc2_w"].reshape(EXPERTS, C, HID // P, P), 3, 0, 2, 1), "fc2_b": turn(a[f + "fc2_b"], 1, 0),
        **shape_constants(),
    }
    nc = bacc.Bacc("TRN2", target_bir_lowering=False, num_devices=1)
    A = {n: nc.dram_tensor(f"in_{n}", v.shape, mybir.dt.from_np(v.dtype), kind="ExternalInput").ap() for n, v in arrays.items()}
    out = nc.dram_tensor("out", (BATCH, N, C), F32, kind="ExternalOutput").ap()
    build(nc, A, out)
    r = run_bass_kernel_spmd(nc, [{f"in_{n}": v for n, v in arrays.items()}], core_ids=[0])
    return r.results[0]["out"]
```

```python
from contextlib import ExitStack
from math import comb, log, pi

import concourse.bass as bass
import numpy as np
from concourse import mybir

ALU = mybir.AluOpType
ACT = mybir.ActivationFunctionType
AX = mybir.AxisListType
F32 = mybir.dt.float32
F16 = mybir.dt.float16
I32 = mybir.dt.int32

BATCH, IMG, FEAT, TXT, C = 8, 1024, 29, 128, 128
N = IMG + TXT
P = 128
KT = N // P
HEADS, DH = 8, 16
VW = DH + 1
QC = 384
NQ = N // QC
KG = 3
UT = 2
HT = NQ * KT
STEP = HT
BH = BATCH * HEADS
EXPERTS, HID, MICRO = 8, 512, 2
SEG = BATCH * N // (MICRO * EXPERTS)
EPS_LN = 1e-5
EPS_ATT = 1e-6
NEAR = 1e-8

DIRICHLET = 6
REACH = 6.25
RMAX = 8.0
DEGREE = 9
RANK = 7
POWERS = 2 * DEGREE
PB = 6
PROWS = PB * DH
LROWS = RANK * DH + 2
PAIRS = DH // 2
WAVES = 2 * 3 * 3
PF = 2 * WAVES
TP = 3
NT = -(-PAIRS // TP)
AROWS = TP * PF
GSCALE = 2.0 ** 14
LSCALE = 2.0 ** 11
MAGIC = 1.5 * 2.0 ** 23
KBASE = 64
PARTS = 3
TROWS = PARTS * DH + 1
TSCALE = 2.0 ** 10
FILLS = 9
RING = 3
LN = 12


def exponent_tables():
    span = 2 * REACH
    t = np.cos(np.pi * (np.arange(4000) + 0.5) / 4000)
    u = (t + 1) / 2 * span * span
    f = 4 * np.log(np.sinc(np.sqrt(u) / DIRICHLET / np.pi))
    cheb = np.polynomial.chebyshev.chebfit(t, f / u, DEGREE - 1)
    poly = np.polynomial.Polynomial(np.polynomial.chebyshev.cheb2poly(cheb))
    coef = poly(np.polynomial.Polynomial([-1, 2])).coef
    both = np.zeros((POWERS + 1, POWERS + 1))
    for m in range(1, DEGREE + 1):
        for i in range(2 * m + 1):
            both[i, 2 * m - i] += span ** 2 * coef[m - 1] / 4 ** m * comb(2 * m, i) * (-1) ** i
    x = np.cos(np.pi * (np.arange(60) + 0.5) / 60)
    grid = x[:, None] ** np.arange(1, POWERS + 1)
    u_, s, v = np.linalg.svd(grid @ both[1:, 1:] @ grid.T)
    left = np.linalg.lstsq(grid, u_[:, :RANK] * np.sqrt(s[:RANK]), rcond=None)[0]
    right = np.linalg.lstsq(grid, v[:RANK].T * np.sqrt(s[:RANK]), rcond=None)[0]
    return left, right, both[1:, 0], both[0, 1:]


def shape_constants():
    position = np.arange(IMG, dtype=np.float32)[:, None]
    div = np.exp(np.arange(0, C, 2, dtype=np.float32) * np.float32(-log(10000.0) / C))
    pe = np.zeros((IMG, C), np.float32)
    pe[:, 0::2] = np.sin(position * div)
    pe[:, 1::2] = np.cos(position * div)
    angles = np.zeros((KBASE + TROWS, NT, AROWS), np.float16)
    for pair in range(PAIRS):
        for w in range(WAVES):
            a, b = (1, 3, 5)[w % 3], (1, 3, 5)[w // 3 % 3] * (1 if w < 9 else -1)
            for phase in range(2):
                col = pair % TP * PF + 2 * w + phase
                for base in (0, KBASE):
                    for part in range(PARTS):
                        angles[base + part * DH + 2 * pair, pair // TP, col] = a / TSCALE
                        angles[base + part * DH + 2 * pair + 1, pair // TP, col] = b / TSCALE
                    angles[base + PARTS * DH, pair // TP, col] = 0.25 * phase
    left, right, own_q, own_k = exponent_tables()
    project = np.zeros((PROWS, 2, POWERS // PB, LROWS))
    for power in range(POWERS):
        for d in range(DH):
            row = power % PB * DH + d
            for side, (table, own) in enumerate(((left, own_q), (right, own_k))):
                for r in range(RANK):
                    project[row, side, power // PB, r * DH + d] = table[power, r] * LSCALE
                project[row, side, power // PB, RANK * DH + side] = own[power] * LSCALE
    lift = np.zeros((LROWS, 2), np.float32)
    lift[RANK * DH + 1, 0] = lift[RANK * DH, 1] = LSCALE
    bits = np.zeros((PROWS, 6), np.float32)
    for row in range(PROWS):
        for b in range(3):
            bits[row, b] = (row // DH + 1) >> b & 1
            bits[row, 3 + b] = 1 - bits[row, b]
    heads = np.kron(np.eye(HEADS), np.ones((1, DH)))
    return {
        "pe": np.ascontiguousarray(pe.reshape(KT - 1, P, C).transpose(1, 0, 2)),
        "angles": angles, "project": project.astype(np.float32), "lift": lift, "bits": bits,
        "ident": np.eye(P, dtype=np.float32), "heads": heads.astype(np.float32),
    }


def tokens_and_qkv(nc, A, S):
    with ExitStack() as ctx:
        sb = lambda name, shape, dt=F32: ctx.enter_context(nc.sbuf_tensor(name, shape, dt))
        sem = lambda name: ctx.enter_context(nc.semaphore(name))
        xT = sb("a_xT", [FEAT, IMG])
        w_tok = sb("a_wtok", [FEAT, C])
        wqkv = sb("a_wqkv", [P, 3 * C])
        pe_sb = sb("a_pe", [P, KT - 1, C])
        ident = sb("a_ident", [P, P])
        h = sb("a_h", [P, 2, KT, C])
        xc = sb("a_xc", [P, KT, C])
        sq = sb("a_sq", [P, KT, C])
        st = sb("a_stat", [P, 6, KT])
        xnT = sb("a_xnT", [P, N])
        qk = sb("a_qk", [P, 2, N])
        va = sb("a_va", [P, HEADS, KT, VW])
        turns = sb("a_turns", [P, 2, N])
        parts = sb("a_parts", [P, PARTS, 2, N], F16)
        r_ = sb("a_r", [P, 2])
        ext = sb("a_ext", [P, 4])
        row = sb("a_row", [1, 8])
        tok_ps = ctx.enter_context(nc.psum_tensor("a_tok_ps", [P, 2, 512], F32))
        x_ps = ctx.enter_context(nc.psum_tensor("a_x_ps", [P, NQ, 512], F32))
        q_ps = ctx.enter_context(nc.psum_tensor("a_q_ps", [P, NQ, 512], F32))
        consts_in, x_in, txt_in = sem("a_consts_in"), sem("a_x_in"), [sem("a_txt_in0"), sem("a_txt_in1")]
        tok_made, h_made, ln, xn_turned, xnT_made = sem("a_tok_made"), sem("a_h_made"), sem("a_ln"), sem("a_xn_turned"), sem("a_xnT_made")
        qkv_made, q_out, k_out, v_out, ones_set = sem("a_qkv_made"), sem("a_q_out"), sem("a_k_out"), sem("a_v_out"), sem("a_ones_set")
        rooted = sem("a_rooted")
        stored, ranged, turned, flagged = sem("a_stored"), sem("a_ranged"), sem("a_turned"), sem("a_flagged")
        split = sem("a_split")
        parts_stored = sem("a_parts_stored")
        STORES = 4
        SPLIT = 5

        tok_flat = tok_ps[:].rearrange("p a (t c) -> p (a t) c", c=C)
        xT_ps = x_ps[:].rearrange("p a (t c) -> p (a t) c", c=C)

        with nc.Block() as block:
            @block.sync
            def _(sp):
                sp.dma_start(w_tok[:], A["tok_w"]).then_inc(consts_in, 16)
                sp.dma_start(wqkv[:], A["wqkvT"]).then_inc(consts_in, 16)
                sp.dma_start(pe_sb[:], A["pe"]).then_inc(consts_in, 16)
                sp.dma_start(ident[:], A["ident"]).then_inc(consts_in, 16)
                sp.dma_start(row[0:1, 0:1], A["R"]).then_inc(consts_in, 16)
                sp.dma_start(r_[:, 0:1], A["R"].to_broadcast([P, 1])).then_inc(consts_in, 16)

                def loads(b, par):
                    if not (type(b) is int and b == 0):
                        sp.wait_ge(tok_made, b)
                    sp.dma_start(xT[:], A["xT"][bass.ds(b, 1)].rearrange("o f s -> (o f) s")).then_inc(x_in, 16)
                    if not (type(b) is int and b < 2):
                        sp.wait_ge(stored, (b - 1) * 16 * STORES)
                    sp.dma_start(h[:, par, KT - 1, :], A["txt"][bass.ds(b, 1)].rearrange("o s c -> (o s) c")).then_inc(txt_in[par], 16)

                def stores(b, par):
                    one = lambda ap: ap[bass.ds(b, 1)]
                    sp.wait_ge(q_out, b + 1)
                    sp.dma_start(one(S["q"]).rearrange("o r n -> (o r) n"), qk[:, 0, :]).then_inc(stored, 16)
                    sp.wait_ge(k_out, b + 1)
                    sp.dma_start(one(S["k"]).rearrange("o r n -> (o r) n"), qk[:, 1, :]).then_inc(stored, 16)
                    sp.dma_start(one(S["h"]).rearrange("o p t c -> (o p) t c"), h[:, par]).then_inc(stored, 16)
                    sp.wait_ge(v_out, b + 1)
                    sp.dma_start(one(S["v"]).rearrange("o h p t v -> p (o h) (t v)"),
                                 va[:].rearrange("p h t v -> p h (t v)")).then_inc(stored, 16)
                    sp.wait_ge(split, SPLIT * (b + 1) + 1)
                    for side in range(2):
                        for part in range(PARTS):
                            sp.dma_start(one(S["parts"][side]).rearrange("o h p d n -> (o h) p d n")[:, part],
                                         parts[:, part, side, :]).then_inc(parts_stored, 16)

                loads(0, 0)
                loads(1, 1)
                stores(0, 0)
                with sp.Fori(0, BATCH // 2 - 1) as i:
                    for n in range(2):
                        b = 2 * i + n + 1
                        loads(b + 1, n)
                        stores(b, 1 - n)
                stores(BATCH - 1, 1)
                sp.wait_ge(stored, BATCH * 16 * STORES)
                sp.wait_ge(parts_stored, BATCH * 16 * 2 * PARTS)
                sp.dma_start(S["h"][BATCH:BATCH + 1], S["h"][0:1]).then_inc(stored, 16)
                for what in ("q", "k"):
                    sp.dma_start(S[what][BATCH:BATCH + 1, 0:2 * DH, :], S[what][0:1, 0:2 * DH, :]).then_inc(stored, 16)
                sp.dma_start(S["v"][BATCH:BATCH + 1, 0:1], S["v"][0:1, 0:1]).then_inc(stored, 16)
                for side in range(2):
                    sp.dma_start(S["parts"][side][BATCH:BATCH + 1, 0:2], S["parts"][side][0:1, 0:2]).then_inc(stored, 16)
                sp.wait_ge(stored, (BATCH * STORES + 6) * 16)

            @block.tensor
            def _(pe):
                pe.wait_ge(consts_in, 6 * 16)

                def front(b):
                    pe.wait_ge(x_in, (b + 1) * 16)
                    if not (type(b) is int and b == 0):
                        pe.wait_ge(h_made, b)
                    for t in range(KT - 1):
                        last = nc.tensor.matmul(tok_flat[:, t, :], xT[:, t * P:(t + 1) * P], w_tok[:], start=True, stop=True)
                    last.then_inc(tok_made, 1)

                def back(b):
                    first = type(b) is int and b == 0
                    pe.wait_ge(ln, (b + 1) * LN)
                    if not first:
                        pe.wait_ge(k_out, b)
                    for t in range(KT):
                        last = nc.tensor.transpose(xT_ps[:, t, :], xc[:, t, :], ident[:])
                    last.then_inc(xn_turned, 1)
                    pe.wait_ge(xnT_made, b + 1)
                    if not first:
                        pe.wait_ge(v_out, b)
                    for i in range(NQ):
                        last = nc.tensor.matmul(q_ps[:, i, 0:QC], wqkv[:, 0:C], xnT[:, i * QC:(i + 1) * QC], start=True, stop=True)
                    last.then_inc(qkv_made, 1)
                    for i in range(NQ):
                        last = nc.tensor.matmul(x_ps[:, i, 0:QC], wqkv[:, C:2 * C], xnT[:, i * QC:(i + 1) * QC], start=True, stop=True)
                    last.then_inc(qkv_made, 1)
                    pe.wait_ge(q_out, b + 1)
                    for t in range(KT):
                        last = nc.tensor.matmul(q_ps[:, t // 3, t % 3 * P:(t % 3 + 1) * P], xnT[:, t * P:(t + 1) * P],
                                                wqkv[:, 2 * C:3 * C], start=True, stop=True)
                    last.then_inc(qkv_made, 1)

                front(0)
                front(1)
                back(0)
                with pe.Fori(1, BATCH - 1) as b:
                    front(b + 1)
                    back(b)
                back(BATCH - 1)
                pe.wait_ge(ranged, 2 * BATCH + 2)
                pe.wait_ge(h_made, BATCH)
                nc.tensor.transpose(tok_flat[0:1, 0, :], ext[:, 0:1], ident[:]).then_inc(turned, 1)

            @block.vector
            def _(dve):
                dve.memset(ext[:], 0.0).then_inc(ranged, 1)
                dve.memset(va[:], 1.0).then_inc(ones_set, 1)
                dve.wait_ge(consts_in, 6 * 16)
                nc.vector.tensor_scalar(r_[:, 1:2], r_[:, 0:1], TSCALE / (2 * pi * DIRICHLET), None, ALU.mult).then_inc(split, 1)

                def front(b, par, half):
                    dve.wait_ge(tok_made, b + 1)
                    if not (type(b) is int and b < 2):
                        dve.wait_ge(stored, (b - 1) * 16 * STORES)
                    nc.vector.tensor_tensor(h[:, par, 0:KT - 1, :], tok_flat[:], pe_sb[:], ALU.add).then_inc(h_made, 1)
                    dve.wait_ge(h_made, b + 1)
                    dve.wait_ge(txt_in[par], (half + 1) * 16)
                    if not (type(b) is int and b == 0):
                        dve.wait_ge(xn_turned, b)
                    layernorm(dve, nc, h[:, par], xc, sq, st, ln, rooted, b * LN, b)

                def back(b):
                    dve.wait_ge(qkv_made, 3 * b + 2)
                    if not (type(b) is int and b == 0):
                        dve.wait_ge(stored, b * 16 * STORES)
                    nc.vector.tensor_copy(qk[:, 1, :].rearrange("p (i n) -> p i n", i=NQ), x_ps[:, :, 0:QC]).then_inc(k_out, 1)
                    dve.wait_ge(k_out, b + 1)
                    dve.wait_ge(q_out, b + 1)
                    flat = qk[:].rearrange("p s n -> p (s n)")
                    nc.vector.tensor_reduce(ext[:, 1:2], flat, AX.X, ALU.max).then_inc(ranged, 1)
                    nc.vector.tensor_reduce(ext[:, 2:3], flat, AX.X, ALU.min).then_inc(ranged, 1)
                    dve.wait_ge(ranged, 2 * b + 3)
                    nc.vector.scalar_tensor_tensor(ext[:, 3:4], ext[:, 2:3], -1.0, ext[:, 1:2], ALU.mult, ALU.max).then_inc(ones_set, 1)
                    dve.wait_ge(ones_set, 2 * b + 2)
                    nc.vector.tensor_tensor(ext[:, 0:1], ext[:, 0:1], ext[:, 3:4], ALU.max).then_inc(ones_set, 1)
                    dve.wait_ge(split, SPLIT * b + 3)
                    nc.vector.tensor_tensor(turns[:], turns[:], parts[:, 0], ALU.subtract).then_inc(split, 1)
                    dve.wait_ge(split, SPLIT * b + 5)
                    nc.vector.tensor_tensor(parts[:, 2], turns[:], parts[:, 1], ALU.subtract).then_inc(split, 1)

                front(0, 0, 0)
                front(1, 1, 0)
                back(0)
                with dve.Fori(0, BATCH // 2 - 1) as i:
                    for n in range(2):
                        b = 2 * i + n + 1
                        front(b + 1, n, i + 1)
                        back(b)
                back(BATCH - 1)
                dve.wait_ge(ones_set, 2 * BATCH + 1)
                dve.drain().then_inc(ranged, 1)
                dve.wait_ge(turned, 1)
                nc.vector.tensor_reduce(row[:, 1:2], tok_flat[0:1, 0, :], AX.X, ALU.max).then_inc(flagged, 1)
                nc.vector.scalar_tensor_tensor(row[:, 2:3], row[:, 0:1], -1.0, row[:, 0:1], ALU.mult, ALU.max).then_inc(flagged, 1)
                dve.wait_ge(flagged, 2)
                nc.vector.tensor_scalar(row[:, 3:4], row[:, 1:2], row[:, 2:3], REACH, ALU.mult, ALU.is_le).then_inc(flagged, 1)
                nc.vector.tensor_scalar(row[:, 4:5], row[:, 2:3], RMAX, None, ALU.is_le).then_inc(flagged, 1)
                dve.wait_ge(flagged, 4)
                nc.vector.tensor_tensor(S["flag"][0:1, 0:1], row[:, 3:4], row[:, 4:5], ALU.mult).then_inc(flagged, 1)
                dve.wait_ge(flagged, 5)

            @block.scalar
            def _(act):
                def back(b, more):
                    first = type(b) is int and b == 0
                    act.wait_ge(xn_turned, b + 1)
                    if not first:
                        act.wait_ge(qkv_made, 3 * b)
                    nc.scalar.activation(xnT[:, 0:1024], x_ps[:, 0:2, :].rearrange("p a n -> p (a n)"), ACT.Copy)
                    nc.scalar.activation(xnT[:, 1024:N], x_ps[:, 2, 0:P], ACT.Copy).then_inc(xnT_made, 1)
                    act.wait_ge(qkv_made, 3 * b + 1)
                    if not first:
                        act.wait_ge(stored, b * 16 * STORES)
                        act.wait_ge(ranged, 2 * b + 1)
                    nc.scalar.activation(qk[:, 0, :].rearrange("p (i n) -> p i n", i=NQ), q_ps[:, :, 0:QC], ACT.Copy).then_inc(q_out, 1)
                    if more:
                        front(b + 1)
                    act.wait_ge(qkv_made, 3 * b + 3)
                    act.wait_ge(ones_set, 1)
                    for i in range(NQ):
                        last = nc.scalar.activation(va[:, :, 3 * i:3 * i + 3, 0:DH],
                                                    q_ps[:, i, 0:QC].rearrange("p (t h d) -> p h t d", t=3, h=HEADS), ACT.Copy)
                    last.then_inc(v_out, 1)
                    act.wait_ge(k_out, b + 1)
                    act.wait_ge(q_out, b + 1)
                    act.wait_ge(split, SPLIT * b + 1)
                    nc.scalar.activation(turns[:], qk[:], ACT.Identity, scale=r_[:, 1:2]).then_inc(split, 1)
                    act.wait_ge(split, SPLIT * b + 2)
                    if not first:
                        act.wait_ge(parts_stored, b * 16 * 2 * PARTS)
                    nc.scalar.activation(parts[:, 0], turns[:], ACT.Copy).then_inc(split, 1)
                    act.wait_ge(split, SPLIT * b + 4)
                    nc.scalar.activation(parts[:, 1], turns[:], ACT.Copy).then_inc(split, 1)

                front = lambda b: layernorm_root(act, nc, st, ln, rooted, b * LN)
                front(0)
                back(0, True)
                with act.Fori(1, BATCH - 1) as b:
                    back(b, True)
                back(BATCH - 1, False)


def layernorm(dve, nc, x, xc, sq, st, done, rooted, at, round_):
    wide = lambda s: st[:, s, :].rearrange("p (t o) -> p t o", o=1).to_broadcast([P, KT, C])
    nc.vector.tensor_reduce(st[:, 0, :], x[:], AX.X, ALU.add).then_inc(done, 1)
    dve.wait_ge(done, at + 1)
    nc.vector.tensor_scalar(st[:, 1, :], st[:, 0, :], 1.0 / C, None, ALU.mult).then_inc(done, 1)
    dve.wait_ge(done, at + 2)
    nc.vector.tensor_tensor(xc[:], x[:], wide(1), ALU.subtract).then_inc(done, 1)
    dve.wait_ge(done, at + 3)
    nc.vector.tensor_tensor(sq[:], xc[:], xc[:], ALU.mult).then_inc(done, 1)
    dve.wait_ge(done, at + 4)
    nc.vector.tensor_reduce(st[:, 2, :], sq[:], AX.X, ALU.add).then_inc(done, 1)
    dve.wait_ge(done, at + 5)
    nc.vector.tensor_scalar(st[:, 3, :], st[:, 2, :], 1.0 / C, EPS_LN, ALU.mult, ALU.add).then_inc(done, 1)
    dve.wait_ge(rooted, round_ + 1)
    nc.vector.reciprocal(st[:, 5, :], st[:, 4, :]).then_inc(done, 1)
    dve.wait_ge(done, at + 7)
    nc.vector.tensor_tensor(st[:, 0, :], st[:, 5, :], st[:, 5, :], ALU.mult).then_inc(done, 1)
    dve.wait_ge(done, at + 8)
    nc.vector.tensor_tensor(st[:, 2, :], st[:, 0, :], st[:, 3, :], ALU.mult).then_inc(done, 1)
    dve.wait_ge(done, at + 9)
    nc.vector.tensor_scalar(st[:, 0, :], st[:, 2, :], -0.5, 1.5, ALU.mult, ALU.add).then_inc(done, 1)
    dve.wait_ge(done, at + 10)
    nc.vector.tensor_tensor(st[:, 1, :], st[:, 5, :], st[:, 0, :], ALU.mult).then_inc(done, 1)
    dve.wait_ge(done, at + 11)
    nc.vector.tensor_tensor(xc[:], xc[:], wide(1), ALU.mult).then_inc(done, 1)


def layernorm_root(act, nc, st, done, rooted, at):
    act.wait_ge(done, at + 6)
    nc.scalar.activation(st[:, 4, :], st[:, 3, :], ACT.Sqrt).then_inc(rooted, 1)


CHAIN = {0: 1, 2: 2, 3: 3, 5: 4, 6: 5, 8: 6}
AHEAD = {1: "exponent", 4: 0, 7: PAIRS - 1}
MULS = len(CHAIN)
WEIGH_PLACES = (3, 7)
WINDOW = STEP // 2
LEAD = 2
WAVE_JOBS = [[("waves", side, t, i) for t in range(NT) for i in range(NQ)] for side in range(2)]
EXP_JOBS = [[("exponent", side, 0, i) for i in range(NQ)] for side in range(2)]
JOBS = dict(zip([(-2, 1), (-2, 2), (-1, 0), (-1, 1), (0, 0), (0, 2), (1, 1), (2, 0), (2, 2)], WAVE_JOBS[0]))
JOBS |= dict(zip([(4, 0), (4, 1), (5, 1)], EXP_JOBS[0]))
JOBS |= dict(zip([(4, 2), (5, 0), (5, 2), (6, 1), (6, 2), (7, 0), (7, 2), (8, 1), (8, 2)], WAVE_JOBS[1]))
JOBS |= dict(zip([(9, 1), (10, 1), (11, 0)], EXP_JOBS[1]))
JOBS = dict(sorted(JOBS.items()))
JPH = len(JOBS)
JOB_AT = {at: i for i, at in enumerate(JOBS)}
WAVE_JPH = 2 * NT * NQ
WAVE_AT = {at: i for i, at in enumerate(at for at in JOBS if JOBS[at][0] == "waves")}
jobs_until = lambda *job: list(JOBS.values()).index(job) + 1
TILE_DONE = {(side, t): jobs_until("waves", side, t, NQ - 1) for side in range(2) for t in range(NT)}
SIDE_DONE = [jobs_until("exponent", side, 0, NQ - 1) for side in range(2)]
JOB_PLACES = (2, 5, 8)
EXP_PLACES = ((2, 2, 2), (5, 5, 5), (8, 8, 8))
JOB_MULS = {"waves": (1, 3, 4), "exponent": (2, 4, 5)}
EXP_THIRDS = {0: 1, 1: 2}
SINES = {(3, 0): (0, 0), (3, 1): (0, 1), (3, 2): (0, 2), (8, 0): (1, 0), (8, 1): (1, 1), (8, 2): (1, 2)}
SPLITS = {(3, 1): (0, 0), (3, 2): (0, 1), (6, 0): (0, 2), (9, 0): (1, 0), (9, 2): (1, 1), (10, 1): (1, 2)}
RESTS = {divmod(3 * v + n + 1, 3): what for (v, n), what in SPLITS.items()}
POWER_STEPS = {(-2, 2): (0, 0), (-1, 0): (0, 1), (-1, 2): (0, 2), (0, 0): (0, 3), (0, 2): (0, 4),
               (5, 0): (1, 0), (5, 1): (1, 1), (5, 2): (1, 2), (6, 0): (1, 3), (7, 0): (1, 4)}
POOL_STEPS = {(0, 0): (0, 0), (0, 1): (0, 1), (1, 1): (0, 2), (2, 0): (0, 3), (3, 0): (0, 4),
              (6, 0): (1, 0), (7, 0): (1, 1), (7, 1): (1, 2), (8, 0): (1, 3), (8, 1): (1, 4)}
SCALED = 7
GNORM = 1.0 / (GSCALE ** 2 * WAVES)
SPREADS = [sum(3 * min(TP, PAIRS - TP * t) for side in range(2) for t in range(NT) if (NT * side + t) % 2 == stage)
           for stage in range(2)]


def spreads_before(h, side, t):
    stage = (NT * side + t) % 2
    return SPREADS[stage] * h + sum(3 * min(TP, PAIRS - TP * b) for a in range(2) for b in range(NT)
                                    if NT * a + b < NT * side + t and (NT * a + b) % 2 == stage)


def tile_of(g):
    return g // HT % 2, g % HT // KT, g % KT


def windows(w):
    return [(o, w - start) for o, start in ((0, 0), (1, WINDOW + 1), (2, STEP)) if -LEAD <= w - start < WINDOW]


def jobs_beside(w, kinds=("waves", "exponent")):
    return [(o, which, JOBS[which][0]) for o, v in windows(w) for which in JOBS if which[0] == v and JOBS[which][0] in kinds]


def fills_before(j, w):
    return FILLS * (STEP * j + w) + len(AHEAD)


def fast_attention(nc, A, S):
    with ExitStack() as ctx:
        sb = lambda name, shape, dt=F32: ctx.enter_context(nc.sbuf_tensor(name, shape, dt))
        sem = lambda name: ctx.enter_context(nc.semaphore(name))
        wq = sb("f_wq", [AROWS, 2, PAIRS, N], F16)
        wk = sb("f_wk", [AROWS, 2, PAIRS, N], F16)
        ex = sb("f_ex", [LROWS, 2, 2, 2, N], F16)
        vv = sb("f_vv", [P, 2, KT, VW])
        xs = sb("f_xs", [PROWS, N])
        x2 = sb("f_x2", [PROWS, N])
        x4 = sb("f_x4", [PROWS, N])
        xb = sb("f_xb", [PROWS, N])
        pw = sb("f_pw", [PROWS, POWERS // PB, N])
        rows = sb("f_rows", [KBASE + TROWS, N], F16)
        near = sb("f_near", [AROWS, QC])
        wave = sb("f_wave", [AROWS, NT, N])
        part = sb("f_part", [AROWS, 2, 2, N], F16)
        prod = sb("f_prod", [P, RING, UT, QC])
        pow4 = sb("f_pow4", [P, RING, UT, QC])
        last = sb("f_last", [P, UT, QC])
        expo = sb("f_expo", [P, RING, UT, QC])
        sums = sb("f_sums", [VW, 2, QC])
        angles = sb("f_angles", [KBASE + TROWS, NT, AROWS], F16)
        project = sb("f_project", [PROWS, 2, POWERS // PB, LROWS])
        lift = sb("f_lift", [LROWS, 2])
        bits = sb("f_bits", [PROWS, 6])
        bits2 = sb("f_bits2", [PROWS, 1])
        r_ = sb("f_r", [P, 8])
        slots = ctx.enter_context(nc.psum_tensor("f_slots", [P, 3, UT, 512], F32))
        av_ps = ctx.enter_context(nc.psum_tensor("f_av_ps", [P, 512], F32))
        feat_ps = ctx.enter_context(nc.psum_tensor("f_feat_ps", [P, 512], F32))

        consts_in, scaled, ones_set = sem("f_consts_in"), sem("f_scaled"), sem("f_ones_set")
        x_in, rows_in = sem("f_x_in"), sem("f_rows_in")
        v_in = [sem("f_v_in0"), sem("f_v_in1")]
        out_stored = [sem("f_out_stored0"), sem("f_out_stored1")]
        spread = [sem("f_spread0"), sem("f_spread1")]
        filled, job_made, job_done = sem("f_filled"), sem("f_job_made"), sem("f_job_done")
        rounded, high_made = sem("f_rounded"), sem("f_high_made")
        powers_a, powers_b, sined, high, rest = sem("f_powers_a"), sem("f_powers_b"), sem("f_sined"), sem("f_high"), sem("f_rest")
        first_copied, last_copied, exped = sem("f_first_copied"), sem("f_last_copied"), sem("f_exped")
        joined, chained, completed, squared, weighed = (sem("f_joined"), sem("f_chained"), sem("f_completed"),
                                                        sem("f_squared"), sem("f_weighed"))
        summed, read_out = sem("f_summed"), sem("f_read_out")

        def freed(eng, j, w, place):
            u = STEP * j + w
            if place < 3 and type(u) is int and u == 0 and place in CHAIN:
                return
            if place == 1:
                eng.wait_ge(last_copied, u + 1)
            elif place == 4:
                eng.wait_ge(exped, u + 2)
            elif place == 7:
                eng.wait_ge(first_copied, u + 2)
            elif place < 3:
                eng.wait_ge(chained, MULS * (u - 1) + list(CHAIN).index(place + 6) + 1)
            else:
                eng.wait_ge(chained, MULS * u + list(CHAIN).index(place - 3) + 1)

        with nc.Block() as block:
            @block.sync
            def _(sp):
                flag = sp.value_load(S["flag"][0:1, 0:1], min_val=0, max_val=1)
                with sp.If(flag > 0):
                    for what, where in (("angles", angles), ("project", project), ("lift", lift), ("bits", bits)):
                        sp.dma_start(where[:], A[what]).then_inc(consts_in, 16)
                    sp.dma_start(r_[:, 0:1], A["R"].to_broadcast([P, 1])).then_inc(consts_in, 16)

                    def head_of(what, h):
                        return S[what].rearrange("b (h d) n -> (b h) d n", d=DH)[bass.ds(h, 1)].rearrange("o d n -> (o d) n")

                    def load_x(h, side, m=None, par=0):
                        if not (type(h) is int and h == 0 and side == 0):
                            sp.wait_ge(powers_b, 5 * (2 * h + side))
                        for b in range(PB):
                            if b == 1 and m is not None:
                                sp.wait_ge(filled, fills_before(m - 1, STEP if par else WINDOW + 1))
                            sp.dma_start(xs[b * DH:(b + 1) * DH, :], head_of("qk"[side], h)).then_inc(x_in, 16)

                    def spread_tile(h, par, side, t):
                        stage = (NT * side + t) % 2
                        sp.wait_ge(rest, 2 * NT * h + NT * side + t + 1)
                        dst = (wq, wk)[side]
                        for pair in range(TP):
                            for place, which in enumerate(((0, 1, 0), (0, 0, 1))[side]):
                                if TP * t + pair < PAIRS:
                                    sp.dma_start(dst[place * PF:(place + 1) * PF, par, TP * t + pair, :],
                                                 part[pair * PF:(pair + 1) * PF, stage, which, :]).then_inc(spread[stage], 16)

                    def load_rows(h):
                        sp.wait_ge(job_made, JPH * (h - 1) + TILE_DONE[1, NT - 1])
                        for side in range(2):
                            sp.dma_start(rows[KBASE * side:KBASE * side + PARTS * DH, :], S["parts"][side].rearrange("b h p d n -> (b h) (p d) n")
                                         [bass.ds(h, 1)].rearrange("o r n -> (o r) n")).then_inc(rows_in, 16)

                    def features(h, m, par, first, stores):
                        if not first:
                            sp.wait_ge(weighed, HT * (h - 1))
                        sp.dma_start(vv[:, par], S["v"].rearrange("b h p t v -> (b h) p t v")[bass.ds(h, 1)]
                                     .rearrange("o p t v -> (o p) t v")).then_inc(v_in[par], 16)
                        stores(0)
                        load_x(h, 1, None if type(m) is int and m == 0 else m, par)
                        for t in range(NT):
                            spread_tile(h, par, 0, t)
                        stores(1)
                        spread_tile(h, par, 1, 0)
                        load_rows(h + 1)
                        spread_tile(h, par, 1, 1)
                        load_x(h + 1, 0)
                        spread_tile(h, par, 1, 2)
                        stores(2)

                    def head(j, hh, first):
                        n = 2 * j + hh
                        def stores(k):
                            if k > 0 or not first:
                                out_group(n, hh, k - 1)
                        features(n + 1, j + hh, (hh + 1) % 2, type(n) is int and n == 0, stores)

                    def out_group(n, hh, i):
                        h, place = (n, i) if i >= 0 else (n - 1, NQ - 1)
                        ring = (NQ * hh + i) % 2
                        sp.wait_ge(read_out, NQ * n + i + 1)
                        sp.dma_start(S["out"].rearrange("b h v n -> (b h) v n")[bass.ds(h, 1)].rearrange("o v n -> (o v) n")
                                     [:, place * QC:(place + 1) * QC], sums[:, ring, :]).then_inc(out_stored[ring], 16)

                    sp.wait_ge(ones_set, 1)
                    for side in range(2):
                        sp.dma_start(rows[KBASE * side:KBASE * side + PARTS * DH, :],
                                     S["parts"][side][0, 0].rearrange("p d n -> (p d) n")).then_inc(rows_in, 16)
                    load_x(0, 0)
                    features(0, 0, 0, True, lambda k: None)
                    head(0, 0, True)
                    head(0, 1, False)
                    with sp.Fori(1, BH // 2) as j:
                        head(j, 0, False)
                        head(j, 1, False)
                    out_group(BH, 0, -1)
                    for ring in range(2):
                        sp.wait_ge(out_stored[ring], 16 * NQ * BH // 2)
                    for stage in range(2):
                        sp.wait_ge(spread[stage], 16 * SPREADS[stage] * (BH + 1))
                    sp.wait_ge(v_in[0], 16 * (BH // 2 + 1))
                    sp.wait_ge(rows_in, 32 * (BH + 2))
                    sp.wait_ge(x_in, 16 * PB * (2 * (BH + 1) + 1))

            @block.tensor
            def _(pe):
                flag = pe.value_load(S["flag"][0:1, 0:1], min_val=0, max_val=1)
                with pe.If(flag > 0):
                    def wave_job(h, which):
                        _, side, t, i = JOBS[which]
                        at = JPH * h + JOB_AT[which]
                        if type(at) is not int or at > 0:
                            pe.wait_ge(job_done, at)
                        pe.wait_ge(rows_in, 32 * (h + 1))
                        base = KBASE * side
                        nc.tensor.matmul(feat_ps[0:AROWS, 0:QC], angles[base:base + TROWS, t, :], rows[base:base + TROWS, i * QC:(i + 1) * QC],
                                         start=True, stop=True).then_inc(job_made, 1)

                    def exponent_part(h, which, k):
                        _, side, _, i = JOBS[which]
                        at = JPH * h + JOB_AT[which]
                        if k == 0:
                            pe.wait_ge(job_done, at)
                            pe.wait_ge(powers_b, 5 * (2 * h + side) + 5)
                        mm = nc.tensor.matmul(feat_ps[0:LROWS, 0:QC], project[:, side, k, :], pw[:, k, i * QC:(i + 1) * QC],
                                              start=(k == 0), stop=(k == POWERS // PB - 1))
                        if k == POWERS // PB - 1:
                            mm.then_inc(job_made, 1)

                    def fill(w, place, what):
                        for k in range(UT):
                            par, qc, tile = tile_of(UT * w + k)
                            q, kt, slot = slice(qc * QC, (qc + 1) * QC), slice(tile * P, (tile + 1) * P), place % 3
                            if what == "exponent":
                                for n, (a, b) in enumerate(((0, 0), (1, 0), (0, 1))):
                                    mm = nc.tensor.matmul(slots[:, slot, k, 0:QC], ex[:, par, 1, b, kt], ex[:, par, 0, a, q],
                                                          start=(n == 0), stop=(n == 2))
                            else:
                                mm = nc.tensor.matmul(slots[:, slot, k, 0:QC], wk[:, par, what, kt], wq[:, par, what, q],
                                                      start=True, stop=True)
                        mm.then_inc(filled, 1)

                    def weigh(j, w, k):
                        g = (UT * w + k) % (2 * HT)
                        par, _, tile = tile_of(g)
                        if k == 0:
                            pe.wait_ge(squared, 2 * (STEP * j + w + 1))
                        if tile == 0 and not (type(j) is int and j == 0 and w == 0):
                            pe.wait_ge(read_out, 2 * NQ * j + (UT * w + k) // KT)
                        nc.tensor.matmul(av_ps[0:VW, 0:QC], vv[:, par, tile, :], pow4[:, w % RING, k, :],
                                         start=(tile == 0), stop=(tile == KT - 1)).then_inc(weighed, 1)

                    pe.wait_ge(consts_in, 16 * 5)
                    pe.wait_ge(scaled, SCALED)
                    for which in JOBS:
                        if JOBS[which][0] == "waves":
                            wave_job(0, which)
                        else:
                            for k in range(POWERS // PB):
                                exponent_part(0, which, k)
                    for which in JOBS:
                        if which[0] < 0:
                            wave_job(1, which)

                    def head_ready(h, m, par):
                        for stage in range(2):
                            pe.wait_ge(spread[stage], 16 * SPREADS[stage] * (h + 1))
                        pe.wait_ge(job_done, JPH * (h + 1))
                        pe.wait_ge(v_in[par], 16 * (m + 1))

                    def step(j, first):
                        for w in range(STEP):
                            for place in range(FILLS):
                                freed(pe, j, w, place)
                                if place in CHAIN:
                                    fill(w, place, CHAIN[place])
                                else:
                                    if place == 1 and w == WINDOW - 1:
                                        head_ready(2 * j + 1, j, 1)
                                    if place == 1 and w == STEP - 1:
                                        head_ready(2 * j + 2, j + 1, 0)
                                    fill((w + 1) % STEP, place, AHEAD[place])
                                for o, which, kind in jobs_beside(w):
                                    if kind == "waves" and place == JOB_PLACES[which[1]]:
                                        wave_job(2 * j + 1 + o, which)
                                    if kind == "exponent":
                                        for k, at in enumerate(EXP_PLACES[which[1]]):
                                            if place == at:
                                                exponent_part(2 * j + 1 + o, which, k)
                                if place in WEIGH_PLACES and not (first and w < 2):
                                    weigh(j, w - 2, WEIGH_PLACES.index(place))

                    head_ready(0, 0, 0)
                    for place in AHEAD:
                        if place == 4:
                            pe.wait_ge(exped, 1)
                        if place == 7:
                            pe.wait_ge(first_copied, 1)
                        fill(0, place, AHEAD[place])
                    step(0, True)
                    with pe.Fori(1, BH // 2) as j:
                        step(j, False)
                    for w in (-2, -1):
                        for k in range(UT):
                            weigh(BH // 2, w, k)

            @block.scalar
            def _(act):
                flag = act.value_load(S["flag"][0:1, 0:1], min_val=0, max_val=1)
                with act.If(flag > 0):
                    def exponent_job(h, par, which):
                        _, side, _, i = JOBS[which]
                        act.wait_ge(job_made, JPH * h + JOB_AT[which] + 1)
                        nc.scalar.activation(ex[:, par, side, 0, i * QC:(i + 1) * QC], feat_ps[0:LROWS, 0:QC], ACT.Identity,
                                             bias=lift[:, side:side + 1]).then_inc(high_made, 1)

                    def power(h, side, n):
                        at = 5 * (2 * h + side)
                        if n == 0:
                            act.wait_ge(x_in, 16 * PB * (2 * h + side + 1))
                            if not (type(at) is int and at == 0):
                                act.wait_ge(powers_b, at)
                            nc.scalar.activation(x2[:], xs[:], ACT.Square, scale=r_[0:PROWS, 1:2]).then_inc(powers_a, 1)
                        elif n == 1:
                            act.wait_ge(powers_a, at + 1)
                            nc.scalar.activation(x4[:], x2[:], ACT.Square).then_inc(powers_a, 1)
                        elif n == 2:
                            nc.scalar.activation(xb[:], x2[:], ACT.Identity, scale=bits[:, 1:2], bias=bits[:, 4:5]).then_inc(powers_a, 1)
                        elif n == 3:
                            if not (type(at) is int and at == 0):
                                act.wait_ge(job_made, JPH * h + (SIDE_DONE[0] if side else 0))
                            nc.scalar.activation(pw[:, 0, :], xs[:], ACT.Identity, scale=bits2[:, 0:1], bias=bits[:, 3:4]).then_inc(powers_a, 1)
                        else:
                            act.wait_ge(powers_a, at + 4)
                            nc.scalar.activation(xs[:], x4[:], ACT.Identity, scale=bits[:, 2:3], bias=bits[:, 5:6]).then_inc(powers_a, 1)

                    def sines(h, side, t):
                        act.wait_ge(job_done, JPH * h + TILE_DONE[side, t])
                        nc.scalar.activation(wave[:, t, :], wave[:, t, :], ACT.Sin, scale=2 * pi).then_inc(sined, 1)

                    def split_high(h, side, t):
                        stage = (NT * side + t) % 2
                        act.wait_ge(sined, 2 * NT * h + NT * side + t + 1)
                        if not (type(h) is int and h == 0 and NT * side + t < 2):
                            act.wait_ge(spread[stage], 16 * spreads_before(h, side, t))
                        nc.scalar.activation(part[:, stage, 0, :], wave[:, t, :], ACT.Copy, scale=GSCALE).then_inc(high, 1)

                    def features(h, par, v, n):
                        if (v, n) in SINES:
                            sines(h, *SINES[v, n])
                        if (v, n) in SPLITS:
                            split_high(h, *SPLITS[v, n])
                        if (v, n) in POWER_STEPS:
                            power(h, *POWER_STEPS[v, n])

                    def ahead(u, w, place):
                        slot = slots[:, place % 3, :, 0:QC]
                        before = type(u) is int
                        if before and u == 0:
                            act.wait_ge(filled, list(AHEAD).index(place) + 1)
                        else:
                            act.wait_ge(filled, fills_before(0, u - 1) + place + 1)
                        if place == 1:
                            if not (before and u < RING):
                                act.wait_ge(completed, u - RING + 1)
                            nc.scalar.activation(expo[:, w % RING], slot, ACT.Exp, scale=0.25 / LSCALE ** 2).then_inc(exped, 1)
                        elif place == 4:
                            if not (before and u < RING):
                                act.wait_ge(squared, 2 * (u - RING) + 1)
                            nc.scalar.activation(prod[:, w % RING], slot, ACT.Copy, scale=GNORM).then_inc(first_copied, 1)
                        else:
                            if not (before and u == 0):
                                act.wait_ge(joined, u)
                            nc.scalar.activation(last[:], slot, ACT.Copy, scale=GNORM).then_inc(last_copied, 1)

                    def square(u, w):
                        act.wait_ge(completed, u + 1)
                        if not (type(u) is int and u < RING):
                            act.wait_ge(weighed, UT * (u - RING + 1))
                        nc.scalar.activation(pow4[:, w % RING], prod[:, w % RING], ACT.Square, scale=r_[:, 3:4]).then_inc(squared, 1)

                    def square_again(u, w):
                        act.wait_ge(squared, 2 * u + 1)
                        nc.scalar.activation(pow4[:, w % RING], pow4[:, w % RING], ACT.Square).then_inc(squared, 1)

                    def read_sums(j, w, k):
                        g = UT * w + k + 1
                        if g % KT:
                            return
                        group = g // KT - 1
                        ring = group % 2
                        act.wait_ge(weighed, 2 * HT * j + g)
                        if not (type(j) is int and j == 0 and group < 2):
                            act.wait_ge(out_stored[ring], 16 * (NQ * j + group // 2))
                        nc.scalar.activation(sums[:, ring, :], av_ps[0:VW, 0:QC], ACT.Copy).then_inc(read_out, 1)

                    act.wait_ge(consts_in, 16 * 5)
                    act.wait_ge(scaled, SCALED)
                    for h in range(2):
                        for v in range(-LEAD, 0 if h else WINDOW):
                            for n in range(3):
                                if (v, n) in JOBS and JOBS[v, n][0] == "exponent":
                                    exponent_job(h, h, (v, n))
                                features(h, h, v, n)
                    for place in AHEAD:
                        ahead(0, 0, place)

                    def step(j, first):
                        for w in range(STEP):
                            u = STEP * j + w
                            for n, place in enumerate(AHEAD):
                                ahead(u + 1, w + 1, place)
                                for o, which, _ in jobs_beside(w, ("exponent",)):
                                    if EXP_THIRDS[which[1]] == n:
                                        exponent_job(2 * j + 1 + o, (1 + o) % 2, which)
                                if n == 0 and not (first and w < 3):
                                    read_sums(j, w - 3, 1)
                                if n == 1 and not (first and w < 2):
                                    read_sums(j, w - 2, 0)
                                if n and not (first and w == 0):
                                    (square, square_again)[n - 1](u - 1, w - 1)
                                for o, v in windows(w):
                                    features(2 * j + 1 + o, (1 + o) % 2, v, n)

                    step(0, True)
                    with act.Fori(1, BH // 2) as j:
                        step(j, False)
                    square(STEP * BH // 2 - 1, -1)
                    square_again(STEP * BH // 2 - 1, -1)
                    read_sums(BH // 2, -1, 1)

            @block.vector
            def _(dve):
                flag = dve.value_load(S["flag"][0:1, 0:1], min_val=0, max_val=1)
                with dve.If(flag > 0):
                    dve.memset(rows[:], 1.0).then_inc(ones_set, 1)
                    dve.memset(r_[:, 4:5], MAGIC).then_inc(scaled, 1)
                    dve.wait_ge(consts_in, 16 * 5)
                    nc.vector.tensor_scalar(r_[:, 1:2], r_[:, 0:1], 1.0 / REACH, None, ALU.mult).then_inc(scaled, 1)
                    for i, (a, b) in enumerate(((0, 2), (2, 5), (5, 6), (6, 3))):
                        nc.vector.tensor_scalar(r_[:, b:b + 1], r_[:, a:a + 1], r_[:, a:a + 1], None, ALU.mult).then_inc(scaled, 1)
                        dve.wait_ge(scaled, i + 3)
                    nc.vector.tensor_scalar(bits2[:, 0:1], bits[:, 0:1], r_[0:PROWS, 1:2], None, ALU.mult).then_inc(scaled, 1)

                    def job(h, par, which):
                        kind, side, t, i = JOBS[which]
                        if kind == "waves":
                            number = WAVE_JPH * h + WAVE_AT[which]
                            dve.wait_ge(job_made, JPH * h + JOB_AT[which] + 1)
                            nc.vector.tensor_scalar(near[:], feat_ps[0:AROWS, 0:QC], MAGIC, None, ALU.add).then_inc(rounded, 1)
                            if not (type(h) is int and h == 0 and side == 0):
                                dve.wait_ge(rest, NT * (2 * h + side - 1) + t + 1)
                            dve.wait_ge(rounded, number + 1)
                            nc.vector.scalar_tensor_tensor(wave[:, t, i * QC:(i + 1) * QC], near[:], MAGIC,
                                                           feat_ps[0:AROWS, 0:QC], ALU.subtract, ALU.subtract).then_inc(job_done, 1)
                        else:
                            dve.wait_ge(high_made, len(EXP_JOBS[0]) * (2 * h + side) + i + 1)
                            nc.vector.scalar_tensor_tensor(ex[:, par, side, 1, i * QC:(i + 1) * QC], feat_ps[0:LROWS, 0:QC],
                                                           lift[:, side:side + 1], ex[:, par, side, 0, i * QC:(i + 1) * QC],
                                                           ALU.add, ALU.subtract).then_inc(job_done, 1)

                    def split_rest(h, side, t):
                        dve.wait_ge(high, 2 * NT * h + NT * side + t + 1)
                        stage = (NT * side + t) % 2
                        nc.vector.scalar_tensor_tensor(part[:, stage, 1, :], wave[:, t, :], GSCALE, part[:, stage, 0, :],
                                                       ALU.mult, ALU.subtract).then_inc(rest, 1)

                    def features(h, v, n):
                        if (v, n) in RESTS:
                            split_rest(h, *RESTS[v, n])

                    for h in range(2):
                        for v in range(-LEAD, 0 if h else WINDOW):
                            for n in range(3):
                                features(h, v, n)
                                if (v, n) in JOBS:
                                    job(h, h, (v, n))

                    def step(j):
                        for w in range(STEP):
                            u = STEP * j + w
                            for c, place in enumerate(CHAIN):
                                if c == 0:
                                    dve.wait_ge(first_copied, u + 1)
                                else:
                                    dve.wait_ge(chained, MULS * u + c)
                                dve.wait_ge(filled, fills_before(j, w) + place + 1)
                                nc.vector.scalar_tensor_tensor(prod[:, w % RING], slots[:, place % 3, :, 0:QC], GNORM,
                                                               prod[:, w % RING], ALU.mult, ALU.mult).then_inc(chained, 1)
                                for o, which, kind in jobs_beside(w):
                                    if c == JOB_MULS[kind][which[1]]:
                                        job(2 * j + 1 + o, (1 + o) % 2, which)
                                for o, v in windows(w):
                                    if c % 2:
                                        features(2 * j + 1 + o, v, c // 2)

                    step(0)
                    with dve.Fori(1, BH // 2) as j:
                        step(j)

            @block.gpsimd
            def _(pool):
                flag = pool.value_load(S["flag"][0:1, 0:1], min_val=0, max_val=1)
                with pool.If(flag > 0):
                    def power(h, side, n):
                        at = 5 * (2 * h + side)
                        if n == 0:
                            pool.wait_ge(powers_a, at + 4)
                            nc.gpsimd.tensor_tensor(pw[:, 0, :], pw[:, 0, :], xb[:], ALU.mult).then_inc(powers_b, 1)
                        elif n == 1:
                            pool.wait_ge(powers_a, at + 5)
                            pool.wait_ge(powers_b, at + 1)
                            nc.gpsimd.tensor_tensor(pw[:, 0, :], pw[:, 0, :], xs[:], ALU.mult).then_inc(powers_b, 1)
                        elif n == 2:
                            nc.gpsimd.tensor_tensor(x2[:], x2[:], x4[:], ALU.mult).then_inc(powers_b, 1)
                        else:
                            pool.wait_ge(powers_b, at + n)
                            nc.gpsimd.tensor_tensor(pw[:, n - 2, :], pw[:, n - 3, :], x2[:], ALU.mult).then_inc(powers_b, 1)

                    def join(u, w):
                        pool.wait_ge(exped, u + 1)
                        pool.wait_ge(last_copied, u + 1)
                        nc.gpsimd.tensor_tensor(expo[:, w % RING], expo[:, w % RING], last[:], ALU.mult).then_inc(joined, 1)

                    def complete(u, w):
                        pool.wait_ge(joined, u + 1)
                        pool.wait_ge(chained, MULS * (u + 1))
                        nc.gpsimd.tensor_tensor(prod[:, w % RING], prod[:, w % RING], expo[:, w % RING], ALU.mult).then_inc(completed, 1)

                    for step_ in POOL_STEPS.values():
                        power(0, *step_)
                    join(0, 0)

                    def step(j, first):
                        for w in range(STEP):
                            for n in range(2):
                                if n == 0 and not (first and w == 0):
                                    complete(STEP * j + w - 1, w - 1)
                                if n == 1:
                                    join(STEP * j + w + 1, w + 1)
                                for o, v in windows(w):
                                    if (v, n) in POOL_STEPS:
                                        power(2 * j + 1 + o, *POOL_STEPS[v, n])

                    step(0, True)
                    with pool.Fori(1, BH // 2) as j:
                        step(j, False)
                    complete(STEP * BH // 2 - 1, -1)


def general_attention(nc, A, S):
    with ExitStack() as ctx:
        sb = lambda name, shape, dt=F32: ctx.enter_context(nc.sbuf_tensor(name, shape, dt))
        sem = lambda name: ctx.enter_context(nc.semaphore(name))
        q_all = sb("g_q", [P, DH, N])
        k_col = sb("g_k", [P, DH])
        v_col = sb("g_v", [P, VW])
        x, dist, turn, half, sine = (sb(f"g_{n}", [P, N]) for n in ("x", "dist", "turn", "half", "sine"))
        num, den, inv, score, weight = (sb(f"g_{n}", [P, N]) for n in ("num", "den", "inv", "score", "weight"))
        acc = sb("g_acc", [VW, N])
        r_ = sb("g_r", [P, 4])
        credit = sb("g_credit", [1, 8])
        sums_ps = ctx.enter_context(nc.psum_tensor("g_sums", [P, NQ, 512], F32))
        r_in, r_made, q_in, kv_in = sem("g_r_in"), sem("g_r_made"), sem("g_q_in"), sem("g_kv_in")
        fun, summed, added, cleared, stored = (sem(f"g_{n}") for n in ("fun", "summed", "added", "cleared", "stored"))
        vec = [sem(f"g_vec{n}") for n in range(4)]
        VEC, FUN = 4 * 7 + 3, 2 * DH + 2

        with nc.Block() as block:
            @block.sync
            def _(sp):
                flag = sp.value_load(S["flag"][0:1, 0:1], min_val=0, max_val=1)
                with sp.If(flag < 1):
                    sp.dma_start(r_[:, 0:1], A["R"].to_broadcast([P, 1])).then_inc(r_in, 16)
                    heads = lambda what, h: S[what].rearrange("b (h d) n -> (b h) d n", d=DH)[bass.ds(h, 1)]
                    with sp.Fori(0, BH) as h:
                        sp.wait_ge(vec[3], h * (KT * VEC) + 1)
                        sp.dma_start(q_all[:], heads("q", h).to_broadcast([P, DH, N])).then_inc(q_in, 16)
                        with sp.Fori(0, KT) as t:
                            sp.wait_ge(summed, h * KT + t + 1)
                            with nc.allow_non_contiguous_dma(reason="keys by rows"):
                                sp.dma_start(k_col[:], heads("k", h).rearrange("o d n -> (o n) d")[bass.ds(t * P, P), :]).then_inc(kv_in, 16)
                            sp.dma_start(v_col[:], S["v"].rearrange("b h p t v -> (b h) t p v")[bass.ds(h, 1), bass.ds(t, 1)]
                                         .rearrange("o t p v -> (o t p) v")).then_inc(kv_in, 16)
                        sp.wait_ge(added, (h + 1) * KT + 1)
                        sp.dma_start(S["out"].rearrange("b h v n -> (b h) v n")[bass.ds(h, 1)].rearrange("o v n -> (o v) n"),
                                     acc[:]).then_inc(stored, 16)
                    sp.wait_ge(stored, 16 * (BH + 1))

            @block.vector
            def _(dve):
                flag = dve.value_load(S["flag"][0:1, 0:1], min_val=0, max_val=1)
                with dve.If(flag < 1):
                    dve.memset(r_[:, 3:4], MAGIC).then_inc(r_made, 1)
                    for n in range(4):
                        dve.memset(credit[:, n:n + 1], 0.0).then_inc(vec[n], 1)
                    dve.memset(credit[:, 4:5], 0.0).then_inc(summed, 1)
                    dve.memset(credit[:, 5:6], 0.0).then_inc(added, 1)
                    dve.memset(credit[:, 6:7], 0.0).then_inc(stored, 16)
                    dve.wait_ge(r_in, 16)
                    nc.vector.scalar_tensor_tensor(r_[:, 1:2], r_[:, 0:1], -1.0, r_[:, 0:1], ALU.mult, ALU.max).then_inc(r_made, 1)
                    dve.wait_ge(r_made, 2)
                    nc.vector.tensor_scalar(r_[:, 2:3], r_[:, 1:2], 1.0 / pi, None, ALU.mult).then_inc(r_made, 1)
                    dve.wait_ge(r_made, 3)
                    with dve.Fori(0, BH) as h:
                        dve.wait_ge(stored, 16 * (h + 1))
                        nc.vector.memset(acc[:], 0.0).then_inc(cleared, 1)
                        with dve.Fori(0, KT) as t:
                            m = h * KT + t
                            dve.wait_ge(cleared, h + 1)
                            dve.wait_ge(q_in, 16 * (h + 1))
                            dve.wait_ge(kv_in, 32 * (m + 1))
                            for d in range(DH):
                                step = vec[d // 4]
                                at, fat = m * VEC + 7 * (d % 4) + 1, m * FUN + 2 * d
                                nc.vector.tensor_scalar(x[:], q_all[:, d, :], k_col[:, d:d + 1], None, ALU.subtract).then_inc(step, 1)
                                dve.wait_ge(step, at + 1)
                                nc.vector.scalar_tensor_tensor(dist[:], x[:], -1.0, x[:], ALU.mult, ALU.max).then_inc(step, 1)
                                dve.wait_ge(step, at + 2)
                                nc.vector.tensor_scalar(dist[:], dist[:], NEAR, None, ALU.max).then_inc(step, 1)
                                dve.wait_ge(fun, fat + 1)
                                nc.vector.tensor_scalar(turn[:], turn[:], MAGIC, None, ALU.subtract).then_inc(step, 1)
                                dve.wait_ge(step, at + 4)
                                nc.vector.scalar_tensor_tensor(half[:], dist[:], r_[:, 2:3], turn[:], ALU.mult, ALU.subtract).then_inc(step, 1)
                                dve.wait_ge(fun, fat + 2)
                                if d % 4 == 0:
                                    nc.vector.tensor_copy(num[:], sine[:]).then_inc(step, 1)
                                    nc.vector.tensor_copy(den[:], dist[:]).then_inc(step, 1)
                                else:
                                    nc.vector.tensor_tensor(num[:], num[:], sine[:], ALU.mult).then_inc(step, 1)
                                    nc.vector.tensor_tensor(den[:], den[:], dist[:], ALU.mult).then_inc(step, 1)
                                if d % 4 == 3:
                                    dve.wait_ge(step, at + 7)
                                    nc.vector.reciprocal(inv[:], den[:]).then_inc(step, 1)
                                    dve.wait_ge(step, at + 8)
                                    nc.vector.tensor_tensor(inv[:], inv[:], num[:], ALU.mult).then_inc(step, 1)
                                    dve.wait_ge(step, at + 9)
                                    if d == 3:
                                        nc.vector.tensor_copy(score[:], inv[:]).then_inc(step, 1)
                                    else:
                                        nc.vector.tensor_tensor(score[:], score[:], inv[:], ALU.mult).then_inc(step, 1)
                                dve.wait_ge(step, at + (10 if d % 4 == 3 else 7))
                            dve.wait_ge(summed, m + 2)
                            nc.vector.tensor_tensor(acc[:].rearrange("v (i n) -> v i n", i=NQ), acc[:].rearrange("v (i n) -> v i n", i=NQ),
                                                    sums_ps[0:VW, :, 0:QC], ALU.add).then_inc(added, 1)
                            dve.wait_ge(added, m + 2)

            @block.scalar
            def _(act):
                flag = act.value_load(S["flag"][0:1, 0:1], min_val=0, max_val=1)
                with act.If(flag < 1):
                    act.wait_ge(r_made, 3)
                    with act.Fori(0, BH) as h:
                        with act.Fori(0, KT) as t:
                            m = h * KT + t
                            for d in range(DH):
                                act.wait_ge(vec[d // 4], m * VEC + 7 * (d % 4) + 4)
                                nc.scalar.activation(turn[:], dist[:], ACT.Identity, scale=r_[:, 2:3], bias=r_[:, 3:4]).then_inc(fun, 1)
                                act.wait_ge(vec[d // 4], m * VEC + 7 * (d % 4) + 6)
                                nc.scalar.activation(sine[:], half[:], ACT.Sin, scale=pi).then_inc(fun, 1)
                            act.wait_ge(vec[3], (m + 1) * VEC + 1)
                            act.wait_ge(summed, m + 1)
                            nc.scalar.activation(weight[:], score[:], ACT.Square).then_inc(fun, 1)
                            act.wait_ge(fun, m * FUN + 2 * DH + 1)
                            nc.scalar.activation(weight[:], weight[:], ACT.Square).then_inc(fun, 1)

            @block.tensor
            def _(pe):
                flag = pe.value_load(S["flag"][0:1, 0:1], min_val=0, max_val=1)
                with pe.If(flag < 1):
                    with pe.Fori(0, BH) as h:
                        with pe.Fori(0, KT) as t:
                            m = h * KT + t
                            pe.wait_ge(fun, (m + 1) * FUN)
                            pe.wait_ge(kv_in, 32 * (m + 1))
                            pe.wait_ge(added, m + 1)
                            for i in range(NQ):
                                mm = nc.tensor.matmul(sums_ps[0:VW, i, 0:QC], v_col[:], weight[:, i * QC:(i + 1) * QC],
                                                      start=True, stop=True)
                            mm.then_inc(summed, 1)


def project_and_ffn(nc, A, S, out):
    with ExitStack() as ctx:
        sb = lambda name, shape, dt=F32: ctx.enter_context(nc.sbuf_tensor(name, shape, dt))
        sem = lambda name: ctx.enter_context(nc.semaphore(name))
        psum = lambda name, shape: ctx.enter_context(nc.psum_tensor(name, shape, F32))
        wproj, wattn, wnext = sb("c_wproj", [P, C]), sb("c_wattn", [P, C]), sb("c_wnext", [P, C])
        rows = sb("c_rows", [1, 3, C])
        cols = sb("c_cols", [P, 3])
        b1, b2 = sb("c_b1", [P, EXPERTS, HID // P]), sb("c_b2", [P, EXPERTS])
        w1, w2 = sb("c_w1", [P, EXPERTS, HID]), sb("c_w2", [P, EXPERTS, HID // P, C])
        ident, heads = sb("c_ident", [P, P]), sb("c_heads", [HEADS, P])
        raw, total, inv = sb("c_raw", [P, 2, N]), sb("c_total", [HEADS, 2, N]), sb("c_inv", [HEADS, N])
        att = sb("c_att", [P, N])
        h = sb("c_h", [P, 2, KT, C])
        x1, x2, sq = sb("c_x1", [P, KT, C]), sb("c_x2", [P, KT, C]), sb("c_sq", [P, KT, C])
        st = sb("c_stat", [P, 6, KT])
        xfT, normT, xaT = sb("c_xfT", [P, N]), sb("c_normT", [P, N]), sb("c_xaT", [P, N])
        hid = sb("c_hid", [P, HID // P, N])
        yT = sb("c_yT", [P, N])
        fin = sb("c_fin", [P, KT, C])
        a_ps, b_ps = psum("c_a", [P, NQ, 512]), psum("c_b", [P, NQ, 512])
        g_ps = psum("c_g", [P, 2, 512])
        consts_in, weights_in, sums_in, h_in, stored = sem("c_consts_in"), sem("c_weights_in"), [sem("c_sums_in0"), sem("c_sums_in1")], [sem("c_h_in0"), sem("c_h_in1")], sem("c_stored")
        ln, rooted, hidden, gelued = (sem(f"c_{n}") for n in ("ln", "rooted", "hidden", "gelued"))
        mm_front, mm_mix, mm_back = sem("c_mm_front"), sem("c_mm_mix"), sem("c_mm_back")
        vec_front, vec_mix, vec_back = sem("c_vec_front"), sem("c_vec_mix"), sem("c_vec_back")
        fun_mix, fun_back = sem("c_fun_mix"), sem("c_fun_back")
        ones_ready, eps_added, copied = sem("c_ones_ready"), sem("c_eps_added"), sem("c_copied")
        a9 = a_ps[:].rearrange("p a n -> p (a n)")[:, 0:N].rearrange("p (t c) -> p t c", c=C)
        b9 = b_ps[:].rearrange("p a n -> p (a n)")[:, 0:N].rearrange("p (t c) -> p t c", c=C)
        a3, b3 = a_ps[:, :, 0:QC], b_ps[:, :, 0:QC]
        by3 = lambda t: t.rearrange("p (i n) -> p i n", i=NQ)
        MMF, MMM, MMB, VF, VM, VB = 2, 3, 2, 3, 2, 3
        NH = SEG // 2
        JOBS_H = 2 * 2 * (HID // P)
        INV_AT, PROJECTION_AT = 10, 14

        with nc.Block() as block:
            @block.sync
            def _(sp):
                for where, what in ((wproj[:], "wprojT"), (wattn[:], "wattnT"), (wnext[:], "wnextT"), (rows[:, 0, :], "b_proj"),
                                    (rows[:, 1, :], "next_b"), (cols[:, 0:1], "ln_g"), (cols[:, 1:2], "ln_b"), (cols[:, 2:3], "attn_b"),
                                    (b1[:], "fc1_b"), (b2[:], "fc2_b"), (ident[:], "ident"),
                                    (heads[:], "heads")):
                    sp.dma_start(where, A[what]).then_inc(consts_in, 16)

                def load(b, par):
                    if type(b) is int and b < 2:
                        pass
                    elif type(b) is int and b == BATCH:
                        sp.wait_ge(copied, 16)
                        sp.wait_ge(vec_back, (b - 1) * VB)
                    else:
                        sp.wait_ge(vec_back, (b - 1) * VB)
                    sp.dma_start(h[:, par], S["h"][bass.ds(b, 1)].rearrange("o p t c -> (o p) t c")).then_inc(h_in[par], 16)
                    sums = S["out"][bass.ds(b, 1)]
                    for k in range(HEADS):
                        sp.dma_start(raw[k * DH:(k + 1) * DH, par, :], sums[:, k, 0:DH, :].rearrange("o v n -> (o v) n")).then_inc(sums_in[par], 16)
                    sp.dma_start(total[:, par, :], sums[:, :, DH, :].rearrange("o h n -> (o h) n")).then_inc(sums_in[par], 16)

                def store(b):
                    sp.wait_ge(vec_back, b * VB + VB)
                    o = out[bass.ds(b, 1)].rearrange("o (t p) c -> p (o t) c", p=P)
                    sp.dma_start(o, fin[:]).then_inc(stored, 16)

                load(0, 0)
                for where, what in ((w1[:], "fc1_wT"), (w2[:], "fc2_wT")):
                    sp.dma_start(where, A[what]).then_inc(weights_in, 16)
                sp.dma_start(S["out"][BATCH:BATCH + 1], S["out"][0:1]).then_inc(copied, 16)
                load(1, 1)
                store(0)
                with sp.Fori(0, BATCH // 2 - 1) as i:
                    for n in range(2):
                        b = 2 * i + n + 1
                        load(b + 1, n)
                        store(b)
                load(BATCH, 0)
                store(BATCH - 1)
                sp.wait_ge(stored, BATCH * 16)
                sp.wait_ge(h_in[0], 16 * (BATCH // 2 + 1))
                sp.wait_ge(sums_in[0], 16 * (HEADS + 1) * (BATCH // 2 + 1))

            @block.tensor
            def _(pe):
                pe.wait_ge(consts_in, 12 * 16)
                pe.wait_ge(ones_ready, 1)

                def turn(src, dst):
                    for t in range(KT):
                        last = nc.tensor.transpose(dst[:, t, :], src[:, t, :], ident[:])
                    return last

                def spread_inv(b):
                    if not (type(b) is int and b == 0):
                        pe.wait_ge(vec_mix, b * VM)
                    pe.wait_ge(vec_front, b * VF + 1)
                    for i in range(NQ):
                        last = nc.tensor.matmul(a3[:, i, :], heads[:], inv[:, i * QC:(i + 1) * QC], start=True, stop=True)
                    last.then_inc(mm_front, 1)

                def projection(b):
                    pe.wait_ge(vec_front, b * VF + 2)
                    for t in range(KT):
                        nc.tensor.matmul(b9[:, t, :], att[:, t * P:(t + 1) * P], wproj[:], start=True, stop=False)
                        last = nc.tensor.matmul(b9[:, t, :], rows[:, 2, :], rows[:, 0, :], start=False, stop=True)
                    last.then_inc(mm_front, 1)

                def mix(b):
                    if not (type(b) is int and b == 0):
                        pe.wait_ge(fun_back, b)
                    pe.wait_ge(ln, (2 * b + 1) * LN)
                    turn(x1, a9).then_inc(mm_mix, 1)
                    pe.wait_ge(ln, (2 * b + 2) * LN)
                    turn(x2, b9).then_inc(mm_mix, 1)
                    pe.wait_ge(fun_mix, b + 1)
                    pe.wait_ge(vec_mix, b * VM + 1)
                    for i in range(NQ):
                        last = nc.tensor.matmul(a3[:, i, :], wattn[:], normT[:, i * QC:(i + 1) * QC], start=True, stop=True)
                    last.then_inc(mm_mix, 1)

                def hidden_part(b, j):
                    pe.wait_ge(weights_in, 2 * 16)
                    pe.wait_ge(vec_mix, b * VM + 2)
                    for e in range(2):
                        for half in range(2):
                            for c in range(HID // P):
                                n = (2 * e + half) * (HID // P) + c
                                lo = e * SEG + half * NH
                                if n == INV_AT:
                                    spread_inv(b + 1)
                                if n == PROJECTION_AT:
                                    projection(b + 1)
                                if n >= 2:
                                    pe.wait_ge(gelued, b * JOBS_H + n - 1)
                                nc.tensor.matmul(g_ps[:, n % 2, 0:NH], w1[:, 2 * j + e, c * P:(c + 1) * P], xaT[:, lo:lo + NH],
                                                 start=True, stop=True).then_inc(hidden, 1)

                def back(b, j):
                    pe.wait_ge(gelued, (b + 1) * JOBS_H)
                    pe.wait_ge(vec_front, (b + 2) * VF)
                    for i in range(4):
                        for c in range(HID // P):
                            last = nc.tensor.matmul((a_ps, b_ps)[i // 2][:, i % 2, 0:NH], w2[:, 2 * j + i // 2, c, :], hid[:, c, i * NH:(i + 1) * NH],
                                                    start=(c == 0), stop=(c == HID // P - 1))
                    last.then_inc(mm_back, 1)
                    pe.wait_ge(vec_back, b * VB + 2)
                    for t in range(KT):
                        nc.tensor.matmul(a9[:, t, :], yT[:, t * P:(t + 1) * P], wnext[:], start=True, stop=False)
                        last = nc.tensor.matmul(a9[:, t, :], rows[:, 2, :], rows[:, 1, :], start=False, stop=True)
                    last.then_inc(mm_back, 1)

                spread_inv(0)
                projection(0)
                mix(0)
                with pe.Fori(0, MICRO) as m:
                    for j in range(BATCH // MICRO):
                        b = m * (BATCH // MICRO) + j
                        hidden_part(b, j)
                        back(b, j)
                        mix(b + 1)

            @block.vector
            def _(dve):
                dve.memset(rows[:, 2, :], 1.0).then_inc(ones_ready, 1)
                dve.wait_ge(consts_in, 12 * 16)

                def front(b, par, half):
                    dve.wait_ge(sums_in[par], (half + 1) * 16 * (HEADS + 1))
                    nc.vector.tensor_scalar(total[:, par, :], total[:, par, :], EPS_ATT, None, ALU.add).then_inc(eps_added, 1)
                    dve.wait_ge(eps_added, b + 1)
                    nc.vector.reciprocal(inv[:], total[:, par, :]).then_inc(vec_front, 1)
                    dve.wait_ge(mm_front, b * MMF + 1)
                    nc.vector.tensor_tensor(by3(att[:]), by3(raw[:, par, :]), a3, ALU.mult).then_inc(vec_front, 1)
                    dve.wait_ge(mm_front, b * MMF + 2)
                    dve.wait_ge(h_in[par], (half + 1) * 16)
                    nc.vector.tensor_tensor(h[:, par], h[:, par], b9, ALU.add).then_inc(vec_front, 1)
                    dve.wait_ge(vec_front, b * VF + 3)
                    layernorm(dve, nc, h[:, par], x1, sq, st, ln, rooted, 2 * b * LN, 2 * b)
                    dve.wait_ge(ln, (2 * b + 1) * LN)
                    layernorm(dve, nc, x1, x2, sq, st, ln, rooted, (2 * b + 1) * LN, 2 * b + 1)

                def mix(b):
                    dve.wait_ge(mm_mix, b * MMM + 1)
                    nc.vector.tensor_copy(xfT[:].rearrange("p (t c) -> p t c", c=C), a9).then_inc(vec_mix, 1)
                    dve.wait_ge(vec_mix, b * VM + 1)
                    dve.wait_ge(mm_mix, b * MMM + 3)
                    nc.vector.scalar_tensor_tensor(by3(xaT[:]), a3, cols[:, 2:3], by3(xfT[:]), ALU.add, ALU.add).then_inc(vec_mix, 1)

                def back(b, j):
                    dve.wait_ge(mm_back, b * MMB + 1)
                    for e in range(2):
                        nc.vector.tensor_scalar(yT[:, e * SEG:(e + 1) * SEG].rearrange("p (i n) -> p i n", i=2), (a_ps, b_ps)[e][:, 0:2, 0:NH],
                                                b2[:, 2 * j + e:2 * j + e + 1], None, ALU.add).then_inc(vec_back, 1)
                    dve.wait_ge(fun_back, b + 1)
                    nc.vector.tensor_tensor(fin[:], fin[:], h[:, j % 2], ALU.add).then_inc(vec_back, 1)

                front(0, 0, 0)
                mix(0)
                with dve.Fori(0, MICRO) as m:
                    for j in range(BATCH // MICRO):
                        b = m * (BATCH // MICRO) + j
                        front(b + 1, (j + 1) % 2, m * (BATCH // MICRO // 2) + (j + 1) // 2)
                        back(b, j)
                        mix(b + 1)

            @block.scalar
            def _(act):
                act.wait_ge(consts_in, 12 * 16)

                def front(b):
                    layernorm_root(act, nc, st, ln, rooted, 2 * b * LN)
                    layernorm_root(act, nc, st, ln, rooted, (2 * b + 1) * LN)

                def mix(b):
                    act.wait_ge(mm_mix, b * MMM + 2)
                    nc.scalar.activation(normT[:].rearrange("p (t c) -> p t c", c=C), b9, ACT.Identity, scale=cols[:, 0:1],
                                         bias=cols[:, 1:2]).then_inc(fun_mix, 1)

                def gelus(b, j):
                    for n in range(JOBS_H):
                        e, half, c = n // (2 * (HID // P)), n // (HID // P) % 2, n % (HID // P)
                        lo = e * SEG + half * NH
                        act.wait_ge(hidden, b * JOBS_H + n + 1)
                        nc.scalar.activation(hid[:, c, lo:lo + NH], g_ps[:, n % 2, 0:NH], ACT.Gelu,
                                             bias=b1[:, 2 * j + e, c:c + 1]).then_inc(gelued, 1)

                def back(b, first):
                    act.wait_ge(mm_back, b * MMB + 2)
                    if not first:
                        act.wait_ge(stored, b * 16)
                    nc.scalar.activation(fin[:], a9, ACT.Gelu).then_inc(fun_back, 1)

                def step(b, j, first):
                    gelus(b, j)
                    front(b + 1)
                    back(b, first)
                    mix(b + 1)

                front(0)
                mix(0)
                for j in range(BATCH // MICRO):
                    step(j, j, j == 0)
                with act.Fori(1, MICRO) as m:
                    for j in range(BATCH // MICRO):
                        step(m * (BATCH // MICRO) + j, j, False)


def build(nc, A, out):
    internal = lambda name, shape, dt=F32: nc.dram_tensor(name, shape, dt, kind="Internal").ap()
    S = {
        "q": internal("s_q", (BATCH + 1, P, N)), "k": internal("s_k", (BATCH + 1, P, N)),
        "v": internal("s_v", (BATCH + 1, HEADS, P, KT, VW)), "h": internal("s_h", (BATCH + 1, P, KT, C)),
        "parts": [internal(f"s_{side}parts", (BATCH + 1, HEADS, PARTS, DH, N), F16) for side in "qk"],
        "out": internal("s_out", (BATCH + 1, HEADS, VW, N)),
    }
    with nc.sbuf_tensor("flag", [1, 1], I32) as flag:
        S["flag"] = flag
        tokens_and_qkv(nc, A, S)
        fast_attention(nc, A, S)
        general_attention(nc, A, S)
    project_and_ffn(nc, A, S, out)


def kernel(**inputs):
    import concourse.bacc as bacc
    import numpy as np
    from concourse import mybir
    from concourse.bass_utils import run_bass_kernel_spmd

    a = {k: np.asarray(v) for k, v in inputs.items()}
    turn = lambda x, *axes: np.ascontiguousarray(np.transpose(x, axes))
    f = "L0_ffn_"
    col = lambda x: np.ascontiguousarray(x.reshape(C, 1))
    arrays = {
        "xT": turn(a["x"].reshape(BATCH, IMG, FEAT), 0, 2, 1), "txt": a["txt"], "tok_w": a["L0_tok_W"],
        "wqkvT": turn(a["L0_attn_w_qkv"], 1, 0), "R": a["L0_attn_paramR"].reshape(1, 1),
        "wprojT": turn(a["L0_attn_w_proj"], 1, 0), "b_proj": a["L0_attn_b_proj"].reshape(1, C),
        "ln_g": col(a[f + "ln_g"]), "ln_b": col(a[f + "ln_b"]), "attn_b": col(a[f + "attn_b"]),
        "wattnT": turn(a[f + "attn_w"], 1, 0), "wnextT": turn(a[f + "next_w"], 1, 0), "next_b": a[f + "next_b"].reshape(1, C),
        "fc1_wT": turn(a[f + "fc1_w"], 2, 0, 1), "fc1_b": turn(a[f + "fc1_b"].reshape(EXPERTS, HID // P, P), 2, 0, 1),
        "fc2_wT": turn(a[f + "fc2_w"].reshape(EXPERTS, C, HID // P, P), 3, 0, 2, 1), "fc2_b": turn(a[f + "fc2_b"], 1, 0),
        **shape_constants(),
    }
    nc = bacc.Bacc("TRN2", target_bir_lowering=False, num_devices=1)
    A = {n: nc.dram_tensor(f"in_{n}", v.shape, mybir.dt.from_np(v.dtype), kind="ExternalInput").ap() for n, v in arrays.items()}
    out = nc.dram_tensor("out", (BATCH, N, C), F32, kind="ExternalOutput").ap()
    build(nc, A, out)
    r = run_bass_kernel_spmd(nc, [{f"in_{n}": v for n, v in arrays.items()}], core_ids=[0])
    return r.results[0]["out"]
```
